# Optimizing a Trainium2 kernel written in Bass

```python
import numpy as np
import jax
import jax.numpy as jnp

def _softmax(x, axis=-1):
    return jax.nn.softmax(x, axis=axis)

def _gelu(x):
    return jax.nn.gelu(x, approximate=True)

def _silu(x):
    return jax.nn.silu(x)

def _sigmoid(x):
    return jax.nn.sigmoid(x)

def _layernorm(x, axis=-1, eps=1e-05):
    m = jnp.mean(x, axis=axis, keepdims=True)
    v = jnp.var(x, axis=axis, keepdims=True)
    return (x - m) / jnp.sqrt(v + eps)

def _scatter_add(tgt, idx, src, axis=0):
    return tgt.at[idx].add(src)

def _segment_sum(src, seg, n):
    return jax.ops.segment_sum(src, seg, n)
kernel_name = 'mk_cond_seq_d1_seqx_r8_c1e380'

def setup_inputs(seed: int=0):
    np.random.seed(seed)
    _w = jnp.asarray

    def _rec_inputs():
        import jax
        import jax.numpy as jnp
        _rk = jax.random.key(seed)
        x = -0.0003929 + 0.9999 * jax.random.normal(jax.random.fold_in(_rk, 1), (32, 32, 256), jnp.float32)
        _lenS = 32 - jax.random.randint(jax.random.fold_in(_rk, 7), (32,), 0, max(1, 32 // 4) + 1, jnp.int32)
        _lenS2 = 32 - jax.random.randint(jax.random.fold_in(_rk, 8), (32,), 0, max(1, 32 // 4) + 1, jnp.int32)
        pos_BxS = jnp.broadcast_to(jnp.arange(32, dtype=jnp.int32), (32, 32))
        cond_2048 = 0.00782532 + 1.00527 * jax.random.normal(jax.random.fold_in(_rk, 12), (32, 256), jnp.float32)
        return (x, pos_BxS, cond_2048)
    x, pos_BxS, cond_2048 = _rec_inputs()

    def _L0_cond_setup():
        import jax, jax.numpy as jnp
        import numpy as np
        HIDDEN, NQ, NKV, HD, INTER = (256, 8, 1, 32, 1024)
        B, S = (4, 256)
        EPS = 1e-06
        ROPE_BASE = 10000.0

        def ada_rms(x, t, w, tw):
            n = x * jax.lax.rsqrt(jnp.mean(jnp.square(x), axis=-1, keepdims=True) + EPS)
            scale = t @ tw.T
            return n * (w * (1.0 + scale))[:, None, :]

        def apply_rope(x, pos_ids):
            half = HD // 2
            inv_freq = 1.0 / ROPE_BASE ** (jnp.arange(0, HD, 2, dtype=jnp.float32) / HD)
            ang = pos_ids.astype(jnp.float32)[:, :, None] * inv_freq
            cos = jnp.concatenate([jnp.cos(ang), jnp.cos(ang)], axis=-1)[:, None]
            sin = jnp.concatenate([jnp.sin(ang), jnp.sin(ang)], axis=-1)[:, None]
            x1, x2 = (x[..., :half], x[..., half:])
            rot = jnp.concatenate([-x2, x1], axis=-1)
            return x * cos + rot * sin
        key = jax.random.key(seed)
        ks = jax.random.split(key, 12)
        f32 = jnp.float32
        inp = {'x': jax.random.normal(ks[0], (B, S, HIDDEN), f32), 'pos_ids': jnp.broadcast_to(jnp.arange(S, dtype=jnp.int32), (B, S)), 'time_emb': jax.random.normal(ks[1], (B, HIDDEN), f32), 'ln1_w': jnp.ones((HIDDEN,), f32), 'ln1_tw': jax.random.normal(ks[2], (HIDDEN, HIDDEN), f32) * 0.02, 'ln2_w': jnp.ones((HIDDEN,), f32), 'ln2_tw': jax.random.normal(ks[3], (HIDDEN, HIDDEN), f32) * 0.02, 'Wq': jax.random.normal(ks[4], (NQ * HD, HIDDEN), f32) * 0.02, 'Wk': jax.random.normal(ks[5], (NKV * HD, HIDDEN), f32) * 0.02, 'Wv': jax.random.normal(ks[6], (NKV * HD, HIDDEN), f32) * 0.02, 'Wo': jax.random.normal(ks[7], (HIDDEN, NQ * HD), f32) * 0.02, 'Wg': jax.random.normal(ks[8], (INTER, HIDDEN), f32) * 0.02, 'Wu': jax.random.normal(ks[9], (INTER, HIDDEN), f32) * 0.02, 'Wd': jax.random.normal(ks[10], (HIDDEN, INTER), f32) * 0.02}
        return inp
    _L0_cond_all = _L0_cond_setup()
    _L0_cond_in = {k: v for k, v in _L0_cond_all.items() if k in ('ln1_w', 'ln1_tw', 'ln2_w', 'ln2_tw', 'Wq', 'Wk', 'Wv', 'Wo', 'Wg', 'Wu', 'Wd')}
    del _L0_cond_all
    return {'x': x, 'pos_BxS': pos_BxS, 'cond_2048': cond_2048, 'L0_cond_ln1_w': _L0_cond_in['ln1_w'], 'L0_cond_ln1_tw': _L0_cond_in['ln1_tw'], 'L0_cond_ln2_w': _L0_cond_in['ln2_w'], 'L0_cond_ln2_tw': _L0_cond_in['ln2_tw'], 'L0_cond_Wq': _L0_cond_in['Wq'], 'L0_cond_Wk': _L0_cond_in['Wk'], 'L0_cond_Wv': _L0_cond_in['Wv'], 'L0_cond_Wo': _L0_cond_in['Wo'], 'L0_cond_Wg': _L0_cond_in['Wg'], 'L0_cond_Wu': _L0_cond_in['Wu'], 'L0_cond_Wd': _L0_cond_in['Wd']}

def reference(x, pos_BxS, cond_2048, L0_cond_ln1_w, L0_cond_ln1_tw, L0_cond_ln2_w, L0_cond_ln2_tw, L0_cond_Wq, L0_cond_Wk, L0_cond_Wv, L0_cond_Wo, L0_cond_Wg, L0_cond_Wu, L0_cond_Wd):
    import jax
    import jax.numpy as jnp

    def _L0_cond_ref(x, pos_ids, time_emb, ln1_w, ln1_tw, ln2_w, ln2_tw, Wq, Wk, Wv, Wo, Wg, Wu, Wd):
        import jax, jax.numpy as jnp
        import numpy as np
        HIDDEN, NQ, NKV, HD, INTER = (256, 8, 1, 32, 1024)
        B, S = (4, 256)
        EPS = 1e-06
        ROPE_BASE = 10000.0

        def ada_rms(x, t, w, tw):
            n = x * jax.lax.rsqrt(jnp.mean(jnp.square(x), axis=-1, keepdims=True) + EPS)
            scale = t @ tw.T
            return n * (w * (1.0 + scale))[:, None, :]

        def apply_rope(x, pos_ids):
            half = HD // 2
            inv_freq = 1.0 / ROPE_BASE ** (jnp.arange(0, HD, 2, dtype=jnp.float32) / HD)
            ang = pos_ids.astype(jnp.float32)[:, :, None] * inv_freq
            cos = jnp.concatenate([jnp.cos(ang), jnp.cos(ang)], axis=-1)[:, None]
            sin = jnp.concatenate([jnp.sin(ang), jnp.sin(ang)], axis=-1)[:, None]
            x1, x2 = (x[..., :half], x[..., half:])
            rot = jnp.concatenate([-x2, x1], axis=-1)
            return x * cos + rot * sin
        b, s, _ = x.shape
        g = NQ // NKV
        res = x
        h = ada_rms(x, time_emb, ln1_w, ln1_tw)
        q = (h @ Wq.T).reshape(b, s, NQ, HD).transpose(0, 2, 1, 3)
        k = (h @ Wk.T).reshape(b, s, NKV, HD).transpose(0, 2, 1, 3)
        v = (h @ Wv.T).reshape(b, s, NKV, HD).transpose(0, 2, 1, 3)
        q = apply_rope(q, pos_ids)
        k = apply_rope(k, pos_ids)
        qg = q.reshape(b, NKV, g, s, HD)
        scores = jnp.einsum('bkgsd,bktd->bkgst', qg, k) / jnp.sqrt(jnp.float32(HD))
        attn = jax.nn.softmax(scores, axis=-1)
        ctx = jnp.einsum('bkgst,bktd->bkgsd', attn, v)
        ctx = ctx.reshape(b, NQ, s, HD).transpose(0, 2, 1, 3).reshape(b, s, NQ * HD)
        x = res + ctx @ Wo.T
        res = x
        h = ada_rms(x, time_emb, ln2_w, ln2_tw)
        mlp = jax.nn.silu(h @ Wg.T) * (h @ Wu.T) @ Wd.T
        return res + mlp
    x = _L0_cond_ref(x, pos_BxS, cond_2048, L0_cond_ln1_w, L0_cond_ln1_tw, L0_cond_ln2_w, L0_cond_ln2_tw, L0_cond_Wq, L0_cond_Wk, L0_cond_Wv, L0_cond_Wo, L0_cond_Wg, L0_cond_Wu, L0_cond_Wd)
    return x

_drawn_inputs = setup_inputs


def setup_inputs(seed=0):
    import zlib

    import numpy as np

    out = dict(_drawn_inputs(seed))
    spreads = {'L0_cond_ln1_w': (1.0, 0.6), 'L0_cond_ln2_w': (1.0, 0.6)}
    factors = {'cond_2048': 2.988,
     'L0_cond_ln1_tw': 8.0,
     'L0_cond_ln2_tw': 3.164,
     'L0_cond_Wq': 8.0,
     'L0_cond_Wk': 8.0,
     'L0_cond_Wv': 2.803,
     'L0_cond_Wo': 2.87}
    for name, (base, spread) in spreads.items():
        noise = np.random.default_rng([zlib.crc32(name.encode()), seed]).standard_normal(out[name].shape)
        drawn = base * np.exp(spread * noise) if base else spread * noise
        out[name] = jnp.asarray(drawn.astype(out[name].dtype))
    for name, factor in factors.items():
        out[name] = (out[name] * factor).astype(out[name].dtype)
    return out
```

```python
from contextlib import ExitStack

import numpy as np
import concourse.bass as bass
from concourse import mybir

F32 = mybir.dt.float32
F32R = mybir.dt.float32r
I32 = mybir.dt.int32
ALU = mybir.AluOpType
ACT = mybir.ActivationFunctionType
AX = mybir.AxisListType

P = 128
BATCH, SEQ, HIDDEN = 32, 32, 256
HEADS, HD, INTER = 8, 32, 1024
TOKENS = BATCH * SEQ
HALF = HD // 2
KH = HIDDEN // P
QK = (HEADS + 1) * HD
QKV = QK + HD
BPT = P // SEQ
TILES = TOKENS // P
CT = 2
GROUPS = TILES // CT
GT = CT * P
GB = CT * BPT
HG = HEADS // BPT
CHUNKS = INTER // P
VB = BPT * HD
GU = 2 * KH * P
EPS = 1e-6
ROPE_BASE = 10000.0
RING = 3

A_COND, A_TW1 = 0, KH * BATCH
A_LN1 = A_TW1 + KH * HIDDEN
A_LN2 = A_LN1 + KH
A_MASK = A_LN2 + KH
A_FREQ = A_MASK + BPT
A_COLS = A_FREQ + HALF
B_ID, B_TW2 = 0, P
B_WO = B_TW2 + KH * HIDDEN
B_COLS = B_WO + HG * HIDDEN

TURN = 2 * np.pi
TURN_1 = 6.28125
TURN_2 = float(np.float32(np.round((TURN - TURN_1) * 2**20) / 2**20))
TURN_3 = float(np.float32(TURN - TURN_1 - TURN_2))
ROUNDER = 1.5 * 2**23
PI_32 = 3.1415925


def block_program(nc, xT, x_tok, pos, pack_a, w_qkv, pack_b, w_gu, w_d, out):
    with ExitStack() as ctx:
        def sb(name, shape, dt=F32):
            return ctx.enter_context(nc.sbuf_tensor(name, shape, dt))

        def sem(name):
            return ctx.enter_context(nc.semaphore(name))

        xt = sb("xt", [P, GROUPS, KH, GT])
        xk = sb("xk", [P, TILES, HIDDEN])
        pos_sb = sb("pos_sb", [P, TILES], I32)
        pa = sb("pa", [P, A_COLS])
        pb = sb("pb", [P, B_COLS])
        wqkv = sb("wqkv", [P, KH, QKV])
        wgu = sb("wgu", [P, CHUNKS, GU])
        wd = sb("wd", [P, CHUNKS, HIDDEN])
        cond = pa[:, A_COND:A_TW1].rearrange("p (k b) -> p k b", k=KH)
        tw1 = pa[:, A_TW1:A_LN1].rearrange("p (k n) -> p k n", k=KH)
        ln = [pa[:, A_LN1:A_LN2], pa[:, A_LN2:A_MASK]]
        mask = pa[:, A_MASK:A_FREQ]
        freq = pa[:, A_FREQ:A_COLS]
        ident = pb[:, B_ID:B_TW2]
        tw2 = pb[:, B_TW2:B_WO].rearrange("p (k n) -> p k n", k=KH)
        wo = pb[:, B_WO:B_COLS].rearrange("p (j n) -> p j n", j=HG)

        wqkv_h, wqkv_l = sb("wqkv_h", [P, KH, QKV], F32R), sb("wqkv_l", [P, KH, QKV], F32R)
        wgu_h, wgu_l = sb("wgu_h", [P, CHUNKS, GU], F32R), sb("wgu_l", [P, CHUNKS, GU], F32R)
        wd_h, wd_l = sb("wd_h", [P, CHUNKS, HIDDEN], F32R), sb("wd_l", [P, CHUNKS, HIDDEN], F32R)

        ang = sb("ang", [P, TILES, HALF])
        turns = sb("turns", [P, TILES, HALF])
        redu = [sb(f"redu{n}", [P, TILES, HALF]) for n in range(4)]
        cos_in = sb("cos_in", [P, TILES, HALF])
        cos = sb("cos", [P, TILES, HALF])
        sin = sb("sin", [P, 2, TILES, HALF])
        mod = [sb(f"mod{n}", [P, KH, BATCH]) for n in range(2)]
        half_neg = sb("half_neg", [P, CT])

        hx = sb("hx", [P, KH, GT])
        hx_h, hx_l = sb("hx_h", [P, KH, GT], F32R), sb("hx_l", [P, KH, GT], F32R)
        sq1, sq2 = sb("sq1", [P, CT, HIDDEN]), sb("sq2", [P, CT, HIDDEN])
        ss1, ms1, rstd1 = (sb(n, [P, CT]) for n in ("ss1", "ms1", "rstd1"))
        cos_r = sb("cos_r", [P, CT, 2, HALF])
        sin_r = sb("sin_r", [P, 2, CT, HALF])
        mask_r = sb("mask_r", [P, CT, BPT])
        rot_a = sb("rot_a", [P, CT, QK])
        rot_b = sb("rot_b", [P, CT, QK])
        qk_rot = sb("qk_rot", [P, CT, QK])
        qkT = sb("qkT", [P, CT, QK])
        kbd = sb("kbd", [P, CT, BPT, SEQ])
        vbd = sb("vbd", [P, CT, VB + BPT])
        top = sb("top", [P, CT * HG * BPT])
        below = sb("below", [P, CT * HG * P])
        prob = sb("prob", [P, CT * HG * P])
        probT = sb("probT", [P, CT * HG * P])
        inv = sb("inv", [P, CT * HG, BPT])
        ctxn = sb("ctxn", [P, CT * HG * P])
        ctxT = sb("ctxT", [P, CT * HG, P])
        ss2, ms2, rstd2 = (sb(n, [P, CT]) for n in ("ss2", "ms2", "rstd2"))
        xn = sb("xn", [P, CT, HIDDEN])
        h2 = sb("h2", [P, KH, GT])
        h2_h = sb("h2_h", [P, GROUPS, KH, GT], F32R)
        h2_l = sb("h2_l", [P, GROUPS, KH, GT], F32R)

        th = sb("th", [P, RING, GT])
        sg = sb("sg", [P, RING, GT])
        hf = sb("hf", [P, CHUNKS, GT])
        hf_h, hf_l = sb("hf_h", [P, CHUNKS, GT], F32R), sb("hf_l", [P, CHUNKS, GT], F32R)

        ps_a = ctx.enter_context(nc.psum_tensor("ps_a", [P, CT, 512], F32))
        ps_s = ctx.enter_context(nc.psum_tensor("ps_s", [P, 512], F32))
        ps_t = ctx.enter_context(nc.psum_tensor("ps_t", [P, 512], F32))
        ps_gu = ctx.enter_context(nc.psum_tensor("ps_gu", [P, RING, 2, GT], F32))
        ps_d = ctx.enter_context(nc.psum_tensor("ps_d", [P, CT, HIDDEN], F32))
        ctx_ps = ps_a[:, :, :].rearrange("p c (j n) -> p (c j) n", j=HG)

        in_pa, in_pos, in_wqkv, in_pb = sem("in_pa"), sem("in_pos"), sem("in_wqkv"), sem("in_pb")
        in_xt = [sem(f"in_xt{n}") for n in range(2)]
        in_xk = [sem(f"in_xk{n}") for n in range(2)]
        in_wgu = [sem(f"in_wgu{n}") for n in range(4)]
        in_wd = [sem(f"in_wd{n}") for n in range(2)]
        out_done = sem("out_done")
        chain = sem("chain")
        half_ready = sem("half_ready")
        sin_ready = sem("sin_ready")
        mod_ps = sem("mod_ps")
        mod_ready = sem("mod_ready")
        ones_ready = sem("ones_ready")
        wqkv_hi, wqkv_lo = sem("wqkv_hi"), sem("wqkv_lo")
        wgu_hi, wgu_lo = sem("wgu_hi"), sem("wgu_lo")
        wd_hi, wd_lo = sem("wd_hi"), sem("wd_lo")
        hx_ready, hx_hi, hx_lo = sem("hx_ready"), sem("hx_hi"), sem("hx_lo")
        ss1_ready, ms1_ready, rstd1_ready = sem("ss1_ready"), sem("ms1_ready"), sem("rstd1_ready")
        tab_ready = sem("tab_ready")
        qkv_ready = sem("qkv_ready")
        rot_ready, qkv_used = sem("rot_ready"), sem("qkv_used")
        qk_ready, qkT_ready, kbd_ready, vbd_ready = sem("qk_ready"), sem("qkT_ready"), sem("kbd_ready"), sem("vbd_ready")
        scores_ready, top_ready, below_ready = sem("scores_ready"), sem("top_ready"), sem("below_ready")
        prob_ready, probT_ps, probT_ready = sem("prob_ready"), sem("probT_ps"), sem("probT_ready")
        ctx_ready, inv_ready, ctxn_ready, ctxT_ready = sem("ctx_ready"), sem("inv_ready"), sem("ctxn_ready"), sem("ctxT_ready")
        proj_ready, x2_ready = sem("proj_ready"), sem("x2_ready")
        ss2_ready, ms2_ready, rstd2_ready = sem("ss2_ready"), sem("ms2_ready"), sem("rstd2_ready")
        xn_ready, xnT_ps = sem("xn_ready"), sem("xnT_ps")
        h2_ready, h2_hi, h2_lo = sem("h2_ready"), sem("h2_hi"), sem("h2_lo")
        gu_ready, th_ready, sg_ready, hf_ready = sem("gu_ready"), sem("th_ready"), sem("sg_ready"), sem("hf_ready")
        hf_hi, hf_lo = sem("hf_hi"), sem("hf_lo")
        down_ready, final_ready = sem("down_ready"), sem("final_ready")

        out_v = out.rearrange("(t p) n -> p t n", p=P)
        block = ctx.enter_context(nc.Block())

        @block.sync
        def _(sp):
            sp.dma_start(pa[:, :], pack_a).then_inc(in_pa, 16)
            sp.dma_start(xt[:, 0], xT[:, 0]).then_inc(in_xt[0], 16)
            sp.dma_start(wqkv[:, :, :], w_qkv).then_inc(in_wqkv, 16)
            sp.dma_start(wgu[:, 0:2, :], w_gu[:, 0:2]).then_inc(in_wgu[0], 16)
            sp.dma_start(pb[:, :], pack_b).then_inc(in_pb, 16)
            for n in range(1, 4):
                sp.dma_start(wgu[:, 2 * n:2 * n + 2, :], w_gu[:, 2 * n:2 * n + 2]).then_inc(in_wgu[n], 16)
            sp.dma_start(xt[:, 1:GROUPS], xT[:, 1:GROUPS]).then_inc(in_xt[1], 16)
            for n in range(2):
                sp.dma_start(wd[:, 4 * n:4 * n + 4, :], w_d[:, 4 * n:4 * n + 4]).then_inc(in_wd[n], 16)
            sp.dma_start(xk[:, CT:TILES, :], x_tok[:, CT:TILES]).then_inc(in_xk[1], 16)
            for g in range(GROUPS - 1):
                sp.wait_ge(final_ready, g + 1)
                sp.dma_start(out_v[:, bass.ds(g * CT, CT), :], xk[:, bass.ds(g * CT, CT), :]).then_inc(out_done, 16)
            for c in range(CT):
                t = TILES - CT + c
                sp.wait_ge(final_ready, GROUPS + c)
                sp.dma_start(out_v[:, t, :], xk[:, t, :]).then_inc(out_done, 16)
            sp.wait_ge(out_done, 16 * (GROUPS - 1 + CT))

        def sums(g, c):
            return ps_s[:, 0:HIDDEN] if g == GROUPS - 1 and c == 1 else ps_d[:, c, :]

        def split_products(pe, ps, lhs_h, lhs_l, rhs_h, rhs_l, first, last):
            pe.matmul(ps, lhs_h, rhs_h, start=first, stop=False)
            pe.matmul(ps, lhs_h, rhs_l, start=False, stop=False)
            return pe.matmul(ps, lhs_l, rhs_h, start=False, stop=last)

        @block.tensor
        def _(pe):
            for n, (w, s, bank) in enumerate(((tw1, in_pa, ps_s), (tw2, in_pb, ps_t))):
                pe.wait_ge(s, 16)
                for f in range(KH):
                    for k in range(KH):
                        mm = pe.matmul(bank[:, f * BATCH:(f + 1) * BATCH], w[:, k, f * P:(f + 1) * P], cond[:, k, :], start=(k == 0), stop=(k == KH - 1))
                mm.then_inc(mod_ps, 1)

            def qkv(g):
                if g == 0:
                    pe.wait_ge(wqkv_hi, 1)
                    pe.wait_ge(wqkv_lo, 1)
                else:
                    pe.wait_ge(ctxn_ready, g)
                pe.wait_ge(hx_hi, g + 1)
                pe.wait_ge(hx_lo, g + 1)
                for c in range(CT):
                    for k in range(KH):
                        sl = slice(c * P, (c + 1) * P)
                        mm = split_products(pe, ps_a[:, c, 0:QKV], hx_h[:, k, sl], hx_l[:, k, sl],
                                            wqkv_h[:, k, :], wqkv_l[:, k, :], k == 0, k == KH - 1)
                mm.then_inc(qkv_ready, 1)

            def scores(g):
                if g == 0:
                    pe.wait_ge(mod_ready, 1)
                else:
                    pe.wait_ge(x2_ready, g)
                pe.wait_ge(kbd_ready, g + 1)
                for c in range(CT):
                    for j in range(HG):
                        at = (c * HG + j) * P
                        mm = pe.matmul(ps_s[:, at:at + P], qkT[:, c, j * P:(j + 1) * P],
                                       kbd[:, c].rearrange("p b t -> p (b t)"), start=True, stop=True)
                mm.then_inc(scores_ready, 1)

            def turn_probs(g):
                pe.wait_ge(prob_ready, g + 1)
                if g:
                    pe.wait_ge(h2_ready, g)
                else:
                    pe.wait_ge(mod_ready, 2)
                for n in range(CT * HG):
                    mm = pe.transpose(ps_t[:, n * P:(n + 1) * P], prob[:, n * P:(n + 1) * P], ident)
                mm.then_inc(probT_ps, 1)

            def context(g):
                pe.wait_ge(probT_ready, g + 1)
                pe.wait_ge(vbd_ready, g + 1)
                pe.wait_ge(ones_ready, 1)
                pe.wait_ge(rot_ready, g + 1)
                for n in range(CT * HG):
                    mm = pe.matmul(ctx_ps[:, n, 0:VB + BPT], probT[:, n * P:(n + 1) * P], vbd[:, n // HG, :],
                                   start=True, stop=True)
                mm.then_inc(ctx_ready, 1)

            def project(g):
                pe.wait_ge(ctxT_ready, g + 1)
                pe.wait_ge(below_ready, g + 1)
                for c in range(CT):
                    for j in range(HG):
                        mm = pe.matmul(ps_s[:, c * HIDDEN:(c + 1) * HIDDEN], ctxT[:, c * HG + j, :], wo[:, j, :],
                                       start=(j == 0), stop=(j == HG - 1))
                mm.then_inc(proj_ready, 1)

            def turn_x(g):
                pe.wait_ge(xn_ready, g + 1)
                pe.wait_ge(probT_ready, g + 1)
                for k in range(KH):
                    for c in range(CT):
                        at = k * GT + c * P
                        mm = pe.transpose(ps_t[:, at:at + P], xn[:, c, k * P:(k + 1) * P], ident)
                mm.then_inc(xnT_ps, 1)

            def gate_up(g, m):
                pe.wait_ge(h2_hi, g + 1)
                pe.wait_ge(h2_lo, g + 1)
                pe.wait_ge(wgu_hi, m // 2 + 1)
                pe.wait_ge(wgu_lo, m // 2 + 1)
                n = g * CHUNKS + m
                if n >= RING:
                    pe.wait_ge(hf_ready, n - RING + 1)
                for part in range(2):
                    for k in range(KH):
                        w = slice((part * KH + k) * P, (part * KH + k + 1) * P)
                        mm = split_products(pe, ps_gu[:, n % RING, part, :], wgu_h[:, m, w], wgu_l[:, m, w],
                                            h2_h[:, g, k, :], h2_l[:, g, k, :], k == 0, k == KH - 1)
                mm.then_inc(gu_ready, 1)

            def down(g, c, m0, m1):
                if m0 == 0 and c == 0 and g:
                    pe.wait_ge(final_ready, g)
                for m in range(m0, m1):
                    pe.wait_ge(wd_hi, m // 4 + 1)
                    pe.wait_ge(wd_lo, m // 4 + 1)
                    pe.wait_ge(hf_hi, g * CHUNKS + m + 1)
                    pe.wait_ge(hf_lo, g * CHUNKS + m + 1)
                    sl = slice(c * P, (c + 1) * P)
                    mm = split_products(pe, sums(g, c), hf_h[:, m, sl], hf_l[:, m, sl], wd_h[:, m, :], wd_l[:, m, :],
                                        m == 0, m == CHUNKS - 1)
                if m1 == CHUNKS:
                    mm.then_inc(down_ready, 1)

            for s in (qkv, scores, turn_probs, context, project, turn_x):
                s(0)
            for g in range(GROUPS - 1):
                qkv(g + 1)
                gate_up(g, 0)
                gate_up(g, 1)
                gate_up(g, 2)
                scores(g + 1)
                gate_up(g, 3)
                gate_up(g, 4)
                turn_probs(g + 1)
                gate_up(g, 5)
                context(g + 1)
                gate_up(g, 6)
                gate_up(g, 7)
                project(g + 1)
                down(g, 0, 0, CHUNKS)
                down(g, 1, 0, 3)
                turn_x(g + 1)
                down(g, 1, 3, CHUNKS)
            g = GROUPS - 1
            for m in range(CHUNKS):
                gate_up(g, m)
            for c in range(CT):
                down(g, c, 0, CHUNKS)

        @block.vector
        def _(dve):
            steps = [0]

            def link(ins):
                steps[0] += 1
                ins.then_inc(chain, 1)
                dve.wait_ge(chain, steps[0])

            dve.memset(half_neg[:, :], -0.5).then_inc(half_ready, 1)

            def modulation(n):
                dve.wait_ge(mod_ps, n + 1)
                bank = (ps_s, ps_t)[n]
                for f in range(KH):
                    ins = dve.tensor_scalar(mod[n][:, f, :], bank[:, f * BATCH:(f + 1) * BATCH], 1.0, ln[n][:, f:f + 1],
                                            ALU.add, ALU.mult)
                ins.then_inc(mod_ready, 1)
                dve.wait_ge(mod_ready, n + 1)

            def per_batch(m, g):
                return m[:, :, bass.ds(g * GB, GB)].unsqueeze(3).broadcast_to([P, KH, GB, SEQ])

            def by_batch(ap):
                return ap.rearrange("p k (b s) -> p k b s", s=SEQ)

            def modulate_x(g):
                if g == 0:
                    dve.wait_ge(in_xt[0], 16)
                else:
                    dve.wait_ge(in_xt[1], 16)
                    dve.wait_ge(hx_hi, g)
                dve.tensor_tensor(by_batch(hx[:, :, :]), by_batch(xt[:, g]), per_batch(mod[0], g),
                                  ALU.mult).then_inc(hx_ready, 1)

            def low_x(g):
                dve.wait_ge(hx_hi, g + 1)
                if g:
                    dve.wait_ge(qkv_ready, g)
                dve.tensor_tensor(hx_l[:, :, :], hx[:, :, :], hx_h[:, :, :].bitcast(F32),
                                  ALU.subtract).then_inc(hx_lo, 1)

            def mean_square_1(g):
                dve.wait_ge(ss1_ready, CT * (g + 1))
                dve.tensor_scalar(ms1[:, :], ss1[:, :], 1.0 / HIDDEN, EPS, ALU.mult, ALU.add).then_inc(ms1_ready, 1)

            def angles():
                dve.wait_ge(in_pos, 16)
                dve.wait_ge(in_pa, 16)
                link(dve.tensor_tensor(ang[:, :, :], pos_sb[:, :].unsqueeze(2).broadcast_to([P, TILES, HALF]),
                                       freq.unsqueeze(1).broadcast_to([P, TILES, HALF]), ALU.mult))
                link(dve.tensor_scalar(redu[3][:, :, :], ang[:, :, :], 1.0 / TURN, ROUNDER, ALU.mult, ALU.add))
                link(dve.tensor_scalar(turns[:, :, :], redu[3][:, :, :], -ROUNDER, None, ALU.add))
                last = ang
                for n, part in enumerate((TURN_1, TURN_2, TURN_3)):
                    link(dve.scalar_tensor_tensor(out=redu[n][:, :, :], in0=turns[:, :, :], scalar=-part,
                                                  in1=last[:, :, :], op0=ALU.mult, op1=ALU.add))
                    last = redu[n]
                link(dve.tensor_scalar(redu[0][:, :, :], redu[2][:, :, :], PI_32, -PI_32, ALU.min, ALU.max))
                link(dve.scalar_tensor_tensor(out=redu[1][:, :, :], in0=redu[0][:, :, :], scalar=-1.0,
                                              in1=redu[0][:, :, :], op0=ALU.mult, op1=ALU.min))
                link(dve.tensor_scalar(cos_in[:, :, :], redu[1][:, :, :], TURN / 4, None, ALU.add))

            def tables(g):
                if g == 0:
                    dve.wait_ge(sin_ready, 3)
                if g:
                    dve.wait_ge(vbd_ready, g)
                dve.wait_ge(rstd1_ready, g + 1)
                r = rstd1[:, :]
                dve.tensor_tensor(cos_r[:, :, :, :],
                                  cos[:, bass.ds(g * CT, CT), :].unsqueeze(2).broadcast_to([P, CT, 2, HALF]),
                                  r.unsqueeze(2).unsqueeze(3).broadcast_to([P, CT, 2, HALF]), ALU.mult)
                dve.tensor_tensor(sin_r[:, :, :, :], sin[:, :, bass.ds(g * CT, CT), :],
                                  r.unsqueeze(1).unsqueeze(3).broadcast_to([P, 2, CT, HALF]), ALU.mult)
                dve.tensor_tensor(mask_r[:, :, :], mask.unsqueeze(1).broadcast_to([P, CT, BPT]),
                                  r.unsqueeze(2).broadcast_to([P, CT, BPT]), ALU.mult).then_inc(tab_ready, 1)

            def rotate(g):
                dve.wait_ge(tab_ready, g + 1)
                dve.wait_ge(qkv_ready, g + 1)
                if g:
                    dve.wait_ge(qk_ready, g)
                q = ps_a[:, :, 0:QK].rearrange("p c (h d) -> p c h d", d=HD)
                a = rot_a[:, :, :].rearrange("p c (h d) -> p c h d", d=HD)
                b = rot_b[:, :, :].rearrange("p c (h d) -> p c h d", d=HD)
                wide = [P, CT, HEADS + 1, HALF]
                for half in range(2):
                    to, frm = slice(half * HALF, (half + 1) * HALF), slice((1 - half) * HALF, (2 - half) * HALF)
                    dve.tensor_tensor(b[:, :, :, to], q[:, :, :, frm],
                                      sin_r[:, half].unsqueeze(2).broadcast_to(wide), ALU.mult)
                dve.tensor_tensor(a, q, cos_r[:, :, :, :].rearrange("p c u d -> p c (u d)").unsqueeze(2)
                                  .broadcast_to([P, CT, HEADS + 1, HD]), ALU.mult).then_inc(rot_ready, 1)

            def add_rotation(g):
                dve.wait_ge(rot_ready, g + 1)
                dve.tensor_tensor(qk_rot[:, :, :], rot_a[:, :, :], rot_b[:, :, :], ALU.add).then_inc(qk_ready, 1)

            def spread_v(g):
                if g:
                    dve.wait_ge(ctx_ready, g)
                v = ps_a[:, :, QK:QKV].unsqueeze(2).broadcast_to([P, CT, BPT, HD])
                dve.tensor_tensor(vbd[:, :, 0:VB].rearrange("p c (b d) -> p c b d", b=BPT), v,
                                  mask_r[:, :, :].unsqueeze(3).broadcast_to([P, CT, BPT, HD]),
                                  ALU.mult).then_inc(vbd_ready, 1)

            def turn_qk(g):
                dve.wait_ge(qk_ready, g + 1)
                if g:
                    dve.wait_ge(scores_ready, g)
                dve.transpose(qkT[:, :, :].rearrange("p c n -> p (c n)"),
                              qk_rot[:, :, :].rearrange("p c n -> p (c n)")).then_inc(qkT_ready, 1)

            def spread_k(g):
                dve.wait_ge(qkT_ready, g + 1)
                dve.tensor_tensor(kbd[:, :, :, :],
                                  qkT[:, :, HEADS * HD:QK].unsqueeze(2).broadcast_to([P, CT, BPT, SEQ]),
                                  mask.unsqueeze(1).unsqueeze(3).broadcast_to([P, CT, BPT, SEQ]),
                                  ALU.mult).then_inc(kbd_ready, 1)

            def take_max(g):
                dve.wait_ge(scores_ready, g + 1)
                s = ps_s[:, :].rearrange("p (n t) -> p n t", t=SEQ)
                dve.tensor_reduce(top[:, :], s, AX.X, ALU.max).then_inc(top_ready, 1)
                dve.wait_ge(top_ready, g + 1)
                if g:
                    dve.wait_ge(prob_ready, g)
                dve.tensor_tensor(below[:, :].rearrange("p (n t) -> p n t", t=SEQ), s,
                                  top[:, :].unsqueeze(2).broadcast_to([P, CT * HG * BPT, SEQ]),
                                  ALU.subtract).then_inc(below_ready, 1)

            def normalise(g):
                dve.wait_ge(ctx_ready, g + 1)
                dve.reciprocal(inv[:, :, :], ctx_ps[:, :, VB:VB + BPT]).then_inc(inv_ready, 1)
                dve.wait_ge(inv_ready, g + 1)
                dve.tensor_tensor(ctxn[:, :].rearrange("p (n b d) -> p n b d", b=BPT, d=HD),
                                  ctx_ps[:, :, 0:VB].rearrange("p n (b d) -> p n b d", d=HD),
                                  inv[:, :, :].unsqueeze(3).broadcast_to([P, CT * HG, BPT, HD]),
                                  ALU.mult).then_inc(ctxn_ready, 1)

            def turn_ctx(g):
                dve.wait_ge(ctxn_ready, g + 1)
                if g:
                    dve.wait_ge(proj_ready, g)
                dve.transpose(ctxT[:, :, :].rearrange("p n t -> p (n t)"), ctxn[:, :]).then_inc(ctxT_ready, 1)

            def add_attention(g):
                dve.wait_ge(proj_ready, g + 1)
                dve.wait_ge(ss1_ready, CT * (g + 1))
                x = xk[:, bass.ds(g * CT, CT), :].rearrange("p c n -> p (c n)")
                dve.tensor_tensor(x, ps_s[:, :], x, ALU.add).then_inc(x2_ready, 1)

            def mean_square_2(g):
                dve.wait_ge(ss2_ready, CT * (g + 1))
                dve.tensor_scalar(ms2[:, :], ss2[:, :], 1.0 / HIDDEN, EPS, ALU.mult, ALU.add).then_inc(ms2_ready, 1)

            def scale_x(g):
                dve.wait_ge(rstd2_ready, g + 1)
                if g:
                    dve.wait_ge(xnT_ps, g)
                for c in range(CT):
                    ins = dve.tensor_scalar(xn[:, c, :], xk[:, g * CT + c, :], rstd2[:, c:c + 1], None, ALU.mult)
                ins.then_inc(xn_ready, 1)

            def modulate_x2(g):
                dve.wait_ge(xnT_ps, g + 1)
                if g:
                    dve.wait_ge(h2_hi, g)
                t = ps_t[:, :].rearrange("p (k n) -> p k n", k=KH)
                dve.tensor_tensor(by_batch(h2[:, :, :]), by_batch(t), per_batch(mod[1], g),
                                  ALU.mult).then_inc(h2_ready, 1)

            def low_x2(g):
                dve.wait_ge(h2_hi, g + 1)
                dve.tensor_tensor(h2_l[:, g], h2[:, :, :], h2_h[:, g].bitcast(F32), ALU.subtract).then_inc(h2_lo, 1)

            def hidden(g, m):
                n = g * CHUNKS + m
                ps = ps_gu[:, n % RING]
                dve.wait_ge(th_ready, n + 1)
                dve.scalar_tensor_tensor(out=sg[:, n % RING], in0=th[:, n % RING], scalar=1.0, in1=ps[:, 0, :],
                                         op0=ALU.add, op1=ALU.mult).then_inc(sg_ready, 1)
                dve.wait_ge(sg_ready, n + 1)
                if g:
                    dve.wait_ge(hf_lo, n - CHUNKS + 1)
                dve.tensor_tensor(hf[:, m], sg[:, n % RING], ps[:, 1, :], ALU.mult).then_inc(hf_ready, 1)

            def finish(g):
                dve.wait_ge(down_ready, CT * (g + 1))
                x = xk[:, bass.ds(g * CT, CT), :]
                dve.scalar_tensor_tensor(out=x, in0=ps_d[:, :, :], scalar=0.5, in1=x,
                                         op0=ALU.mult, op1=ALU.add).then_inc(final_ready, 1)

            def finish_last(c):
                t = TILES - CT + c
                dve.wait_ge(down_ready, t + 1)
                dve.scalar_tensor_tensor(out=xk[:, t, :], in0=sums(GROUPS - 1, c), scalar=0.5, in1=xk[:, t, :],
                                         op0=ALU.mult, op1=ALU.add).then_inc(final_ready, 1)

            angles()
            modulation(0)
            modulate_x(0)
            dve.wait_ge(wqkv_hi, 1)
            dve.tensor_tensor(wqkv_l[:, :, :], wqkv[:, :, :], wqkv_h[:, :, :].bitcast(F32),
                              ALU.subtract).then_inc(wqkv_lo, 1)
            low_x(0)
            mean_square_1(0)
            dve.tensor_copy(vbd[:, :, VB:VB + BPT], mask.unsqueeze(1).broadcast_to([P, CT, BPT])).then_inc(ones_ready, 1)
            modulation(1)
            tables(0)
            for s in (rotate, add_rotation, spread_v, turn_qk, spread_k, take_max, normalise, turn_ctx,
                      add_attention, mean_square_2, scale_x, modulate_x2, low_x2):
                s(0)
            modulate_x(1)
            low_x(1)
            mean_square_1(1)
            tables(1)
            for g in range(GROUPS - 1):
                n = g + 1
                rotate(n)
                hidden(g, 0)
                add_rotation(n)
                spread_v(n)
                hidden(g, 1)
                turn_qk(n)
                spread_k(n)
                hidden(g, 2)
                hidden(g, 3)
                take_max(n)
                hidden(g, 4)
                hidden(g, 5)
                normalise(n)
                turn_ctx(n)
                hidden(g, 6)
                hidden(g, 7)
                add_attention(n)
                mean_square_2(n)
                if n + 1 < GROUPS:
                    modulate_x(n + 1)
                    low_x(n + 1)
                scale_x(n)
                modulate_x2(n)
                low_x2(n)
                if n + 1 < GROUPS:
                    mean_square_1(n + 1)
                    tables(n + 1)
                finish(g)
            g = GROUPS - 1
            for m in range(CHUNKS):
                hidden(g, m)
            for c in range(CT):
                finish_last(c)

        @block.scalar
        def _(act):
            act.dma_start(xk[:, 0:CT, :], x_tok[:, 0:CT]).then_inc(in_xk[0], 16)
            act.dma_start(pos_sb[:, :], pos).then_inc(in_pos, 16)

            def squares_1(g):
                if g == 0:
                    act.wait_ge(in_xk[0], 16)
                else:
                    act.wait_ge(in_xk[1], 16)
                    act.wait_ge(ms1_ready, g)
                for c in range(CT):
                    act.activation(sq1[:, c, :], xk[:, g * CT + c, :], ACT.Square,
                                   accum_out=ss1[:, c:c + 1]).then_inc(ss1_ready, 1)

            def squares_2(g):
                act.wait_ge(x2_ready, g + 1)
                for c in range(CT):
                    act.activation(sq2[:, c, :], xk[:, g * CT + c, :], ACT.Square,
                                   accum_out=ss2[:, c:c + 1]).then_inc(ss2_ready, 1)

            def high_x(g):
                act.wait_ge(hx_ready, g + 1)
                if g:
                    act.wait_ge(qkv_ready, g)
                    act.wait_ge(hx_lo, g)
                act.activation(hx_h[:, :, :], hx[:, :, :], ACT.Copy).then_inc(hx_hi, 1)

            def high_x2(g):
                act.wait_ge(h2_ready, g + 1)
                act.activation(h2_h[:, g], h2[:, :, :], ACT.Copy).then_inc(h2_hi, 1)

            def exps(g):
                act.wait_ge(below_ready, g + 1)
                if g:
                    act.wait_ge(probT_ps, g)
                act.activation(prob[:, :], below[:, :], ACT.Exp, scale=float(HD) ** -0.5).then_inc(prob_ready, 1)

            def copy_probT(g):
                act.wait_ge(probT_ps, g + 1)
                if g:
                    act.wait_ge(ctx_ready, g)
                act.activation(probT[:, :], ps_t[:, :], ACT.Copy).then_inc(probT_ready, 1)

            def tanh(g, m):
                n = g * CHUNKS + m
                act.wait_ge(gu_ready, n + 1)
                if n >= RING:
                    act.wait_ge(sg_ready, n - RING + 1)
                act.activation(th[:, n % RING], ps_gu[:, n % RING, 0, :], ACT.Tanh, scale=0.5).then_inc(th_ready, 1)

            def high_hidden(g, m):
                n = g * CHUNKS + m
                act.wait_ge(hf_ready, n + 1)
                if g:
                    act.wait_ge(down_ready, CT * g)
                act.activation(hf_h[:, m], hf[:, m], ACT.Copy).then_inc(hf_hi, 1)

            def high_gu(n):
                act.wait_ge(in_wgu[n], 16)
                act.activation(wgu_h[:, 2 * n:2 * n + 2, :], wgu[:, 2 * n:2 * n + 2, :], ACT.Copy).then_inc(wgu_hi, 1)

            act.wait_ge(in_wqkv, 16)
            act.activation(wqkv_h[:, :, :], wqkv[:, :, :], ACT.Copy).then_inc(wqkv_hi, 1)
            act.wait_ge(chain, 7)
            for half, sign in enumerate((-1.0, 1.0)):
                act.activation(sin[:, half], redu[0][:, :, :], ACT.Sin, scale=sign).then_inc(sin_ready, 1)
            squares_1(0)
            high_x(0)
            act.wait_ge(chain, 9)
            act.activation(cos[:, :, :], cos_in[:, :, :], ACT.Sin).then_inc(sin_ready, 1)
            high_gu(0)
            exps(0)
            high_gu(1)
            copy_probT(0)
            high_gu(2)
            high_gu(3)
            squares_2(0)
            squares_1(1)
            high_x2(0)
            high_x(1)
            for n in range(2):
                act.wait_ge(in_wd[n], 16)
                act.activation(wd_h[:, 4 * n:4 * n + 4, :], wd[:, 4 * n:4 * n + 4, :], ACT.Copy).then_inc(wd_hi, 1)
            for g in range(GROUPS - 1):
                n = g + 1
                tanh(g, 0)
                tanh(g, 1)
                high_hidden(g, 0)
                tanh(g, 2)
                high_hidden(g, 1)
                tanh(g, 3)
                high_hidden(g, 2)
                exps(n)
                tanh(g, 4)
                high_hidden(g, 3)
                copy_probT(n)
                tanh(g, 5)
                high_hidden(g, 4)
                tanh(g, 6)
                high_hidden(g, 5)
                tanh(g, 7)
                high_hidden(g, 6)
                high_hidden(g, 7)
                squares_2(n)
                if n + 1 < GROUPS:
                    high_x(n + 1)
                    squares_1(n + 1)
                high_x2(n)
            g = GROUPS - 1
            for m in range(CHUNKS):
                tanh(g, m)
                if m:
                    high_hidden(g, m - 1)
            high_hidden(g, CHUNKS - 1)

        @block.gpsimd
        def _(pool):
            def power_1(g):
                pool.wait_ge(ms1_ready, g + 1)
                if g:
                    pool.wait_ge(tab_ready, g)
                pool.tensor_tensor(rstd1[:, :], ms1[:, :], half_neg[:, :], ALU.pow).then_inc(rstd1_ready, 1)

            def power_2(g):
                pool.wait_ge(ms2_ready, g + 1)
                if g:
                    pool.wait_ge(xn_ready, g)
                pool.tensor_tensor(rstd2[:, :], ms2[:, :], half_neg[:, :], ALU.pow).then_inc(rstd2_ready, 1)

            def low_hidden(g, m):
                n = g * CHUNKS + m
                pool.wait_ge(hf_hi, n + 1)
                pool.tensor_tensor(hf_l[:, m], hf[:, m], hf_h[:, m].bitcast(F32), ALU.subtract).then_inc(hf_lo, 1)

            def low_gu(n):
                sl = slice(2 * n, 2 * n + 2)
                pool.wait_ge(wgu_hi, n + 1)
                pool.tensor_tensor(wgu_l[:, sl, :], wgu[:, sl, :], wgu_h[:, sl, :].bitcast(F32),
                                   ALU.subtract).then_inc(wgu_lo, 1)

            pool.wait_ge(half_ready, 1)
            power_1(0)
            for n in range(4):
                low_gu(n)
            power_2(0)
            power_1(1)
            for n in range(2):
                sl = slice(4 * n, 4 * n + 4)
                pool.wait_ge(wd_hi, n + 1)
                pool.tensor_tensor(wd_l[:, sl, :], wd[:, sl, :], wd_h[:, sl, :].bitcast(F32),
                                   ALU.subtract).then_inc(wd_lo, 1)
            for g in range(GROUPS - 1):
                n = g + 1
                for m in range(CHUNKS):
                    low_hidden(g, m)
                power_2(n)
                if n + 1 < GROUPS:
                    power_1(n + 1)
            for m in range(CHUNKS):
                low_hidden(GROUPS - 1, m)


def kernel(**inputs):
    import concourse.bacc as bacc
    from concourse.bass_utils import run_bass_kernel_spmd as run

    a = {n.replace("L0_cond_", ""): np.ascontiguousarray(v) for n, v in inputs.items()}

    def rows(w, parts):
        return w.reshape(parts, P, -1).transpose(1, 0, 2)

    x2d = a["x"].reshape(TOKENS, HIDDEN)
    xT = x2d.T.reshape(KH, P, GROUPS, GT).transpose(1, 2, 0, 3)
    x_tok = rows(x2d, TILES)
    pos = a["pos_BxS"].reshape(TILES, P).T
    batch_of = np.arange(P) // SEQ
    mask = (batch_of[:, None] == np.arange(BPT)[None, :]).astype(np.float32)
    exponent = np.arange(0, HD, 2, dtype=np.float32) / np.float32(HD)
    freq = np.broadcast_to(np.float32(1.0) / np.float32(ROPE_BASE) ** exponent, (P, HALF))
    pack_a = np.concatenate([rows(a["cond_2048"].T, KH).reshape(P, -1), rows(a["ln1_tw"].T, KH).reshape(P, -1),
                             a["ln1_w"].reshape(KH, P).T, a["ln2_w"].reshape(KH, P).T, mask, freq], axis=1)
    w_qkv = rows(np.concatenate([a["Wq"], a["Wk"], a["Wv"]], axis=0).T, KH)
    pack_b = np.concatenate([np.eye(P, dtype=np.float32), rows(a["ln2_tw"].T, KH).reshape(P, -1),
                             rows(a["Wo"].T, HG).reshape(P, -1)], axis=1)
    w_gu = np.stack([a["Wg"], a["Wu"]]).reshape(2, CHUNKS, P, KH, P).transpose(4, 1, 0, 3, 2).reshape(P, CHUNKS, GU)
    w_d = rows(a["Wd"].T, CHUNKS)

    nc = bacc.Bacc("TRN2", target_bir_lowering=False, num_devices=1)
    arrays, args = {}, []
    for name, v in (("xT", xT), ("x_tok", x_tok), ("pos", pos), ("pack_a", pack_a), ("w_qkv", w_qkv),
                    ("pack_b", pack_b), ("w_gu", w_gu), ("w_d", w_d)):
        v = np.ascontiguousarray(v)
        arrays["in_" + name] = v
        args.append(nc.dram_tensor("in_" + name, v.shape, mybir.dt.from_np(v.dtype), kind="ExternalInput").ap())
    args.append(nc.dram_tensor("out_x", (TOKENS, HIDDEN), F32, kind="ExternalOutput").ap())
    block_program(nc, *args)
    r = run(nc, [arrays], core_ids=[0])
    return r.results[0]["out_x"].reshape(BATCH, SEQ, HIDDEN)
```

```python
from contextlib import ExitStack

import numpy as np
import concourse.bass as bass
from concourse import mybir

F32 = mybir.dt.float32
F32R = mybir.dt.float32r
I32 = mybir.dt.int32
ALU = mybir.AluOpType
ACT = mybir.ActivationFunctionType
AX = mybir.AxisListType

P = 128
BATCH, SEQ, HIDDEN = 32, 32, 256
HEADS, HD, INTER = 8, 32, 1024
TOKENS = BATCH * SEQ
HALF = HD // 2
KH = HIDDEN // P
QK = (HEADS + 1) * HD
QKV = QK + HD
BPT = P // SEQ
TILES = TOKENS // P
CT = 2
GROUPS = TILES // CT
GT = CT * P
GB = CT * BPT
HG = HEADS // BPT
CHUNKS = INTER // P
VB = BPT * HD
GU = 2 * KH * P
EPS = 1e-6
ROPE_BASE = 10000.0
RING = 3

A_COND, A_TW1 = 0, KH * BATCH
A_COLS = A_TW1 + KH * HIDDEN
S_LN1, S_LN2 = 0, KH
S_MASK = S_LN2 + KH
S_FREQ = S_MASK + BPT
S_COLS = S_FREQ + HALF
B_ID, B_TW2 = 0, P
B_WO = B_TW2 + KH * HIDDEN
B_COLS = B_WO + HG * HIDDEN

TURN = 2 * np.pi
TURN_1 = 6.28125
TURN_2 = float(np.float32(TURN - TURN_1))
ROUNDER = 1.5 * 2**23
PI_32 = 3.1415925


def block_program(nc, xT, x_tok, pos, pack_s, pack_a, w_qkv, pack_b, w_gu, w_d, out):
    with ExitStack() as ctx:
        def sb(name, shape, dt=F32):
            return ctx.enter_context(nc.sbuf_tensor(name, shape, dt))

        def sem(name):
            return ctx.enter_context(nc.semaphore(name))

        xt = sb("xt", [P, GROUPS, KH, GT])
        xk = sb("xk", [P, TILES, HIDDEN])
        pos_sb = sb("pos_sb", [P, TILES], I32)
        small = sb("small", [P, S_COLS])
        pa = sb("pa", [P, A_COLS])
        pb = sb("pb", [P, B_COLS])
        wqkv = sb("wqkv", [P, KH, QKV])
        wgu = sb("wgu", [P, CHUNKS, GU])
        wd = sb("wd", [P, CHUNKS, HIDDEN])
        cond = pa[:, A_COND:A_TW1].rearrange("p (k b) -> p k b", k=KH)
        tw1 = pa[:, A_TW1:A_COLS].rearrange("p (k n) -> p k n", k=KH)
        ln = [small[:, S_LN1:S_LN2], small[:, S_LN2:S_MASK]]
        mask = small[:, S_MASK:S_FREQ]
        freq = small[:, S_FREQ:S_COLS]
        ident = pb[:, B_ID:B_TW2]
        tw2 = pb[:, B_TW2:B_WO].rearrange("p (k n) -> p k n", k=KH)
        wo = pb[:, B_WO:B_COLS].rearrange("p (j n) -> p j n", j=HG)

        wqkv_h, wqkv_l = sb("wqkv_h", [P, KH, QKV], F32R), sb("wqkv_l", [P, KH, QKV], F32R)
        wgu_h, wgu_l = sb("wgu_h", [P, CHUNKS, GU], F32R), sb("wgu_l", [P, CHUNKS, GU], F32R)
        wd_h, wd_l = sb("wd_h", [P, CHUNKS, HIDDEN], F32R), sb("wd_l", [P, CHUNKS, HIDDEN], F32R)

        ang = sb("ang", [P, TILES, HALF])
        turns = sb("turns", [P, TILES, HALF])
        redu = [sb(f"redu{n}", [P, TILES, HALF]) for n in range(3)]
        sin_in = sb("sin_in", [P, TILES, HALF])
        cos_in = sb("cos_in", [P, TILES, HALF])
        cos = sb("cos", [P, TILES, HALF])
        sin = sb("sin", [P, 2, TILES, HALF])
        mod = [sb(f"mod{n}", [P, KH, BATCH]) for n in range(2)]
        half_neg = sb("half_neg", [P, CT])

        hx = sb("hx", [P, KH, GT])
        hx_h, hx_l = sb("hx_h", [P, KH, GT], F32R), sb("hx_l", [P, KH, GT], F32R)
        sq1, sq2 = sb("sq1", [P, CT, HIDDEN]), sb("sq2", [P, CT, HIDDEN])
        ss1, ms1, rstd1 = (sb(n, [P, CT]) for n in ("ss1", "ms1", "rstd1"))
        cos_r = sb("cos_r", [P, CT, 2, HALF])
        sin_r = sb("sin_r", [P, 2, CT, HALF])
        mask_r = sb("mask_r", [P, CT, BPT])
        rot_a = sb("rot_a", [P, CT, QK])
        rot_b = sb("rot_b", [P, CT, QK])
        qk_rot = sb("qk_rot", [P, CT, QK])
        qkT = sb("qkT", [P, CT, QK])
        kbd = sb("kbd", [P, CT, BPT, SEQ])
        vbd = sb("vbd", [P, CT, VB + BPT])
        top = sb("top", [P, CT * HG * BPT])
        below = sb("below", [P, CT * HG * P])
        prob = sb("prob", [P, CT * HG * P])
        probT = sb("probT", [P, CT * HG * P])
        inv = sb("inv", [P, CT * HG, BPT])
        ctxn = sb("ctxn", [P, CT * HG * P])
        ctxT = sb("ctxT", [P, CT * HG, P])
        ss2, ms2, rstd2 = (sb(n, [P, CT]) for n in ("ss2", "ms2", "rstd2"))
        xn = sb("xn", [P, CT, HIDDEN])
        h2 = sb("h2", [P, KH, GT])
        h2_h = sb("h2_h", [P, GROUPS, KH, GT], F32R)
        h2_l = sb("h2_l", [P, GROUPS, KH, GT], F32R)

        th = sb("th", [P, RING, GT])
        sg = sb("sg", [P, RING, GT])
        hf = sb("hf", [P, CHUNKS, GT])
        hf_h, hf_l = sb("hf_h", [P, CHUNKS, GT], F32R), sb("hf_l", [P, CHUNKS, GT], F32R)

        ps_a = ctx.enter_context(nc.psum_tensor("ps_a", [P, CT, 512], F32))
        ps_s = ctx.enter_context(nc.psum_tensor("ps_s", [P, 512], F32))
        ps_t = ctx.enter_context(nc.psum_tensor("ps_t", [P, 512], F32))
        ps_gu = ctx.enter_context(nc.psum_tensor("ps_gu", [P, RING, 2, GT], F32))
        ps_d = ctx.enter_context(nc.psum_tensor("ps_d", [P, CT, HIDDEN], F32))
        ctx_ps = ps_a[:, :, :].rearrange("p c (j n) -> p (c j) n", j=HG)

        in_small, in_pos, in_pa, in_wqkv, in_pb = (sem(n) for n in ("in_small", "in_pos", "in_pa", "in_wqkv", "in_pb"))
        in_xt = [sem(f"in_xt{n}") for n in range(2)]
        in_xk = [sem(f"in_xk{n}") for n in range(2)]
        in_wgu = [sem(f"in_wgu{n}") for n in range(4)]
        in_wd = [sem(f"in_wd{n}") for n in range(2)]
        out_done = sem("out_done")
        chain = sem("chain")
        half_ready = sem("half_ready")
        sin_ready = sem("sin_ready")
        mod_ps = sem("mod_ps")
        mod_ready = sem("mod_ready")
        ones_ready = sem("ones_ready")
        wqkv_hi, wqkv_lo = sem("wqkv_hi"), sem("wqkv_lo")
        wgu_hi, wgu_lo = sem("wgu_hi"), sem("wgu_lo")
        wd_hi, wd_lo = sem("wd_hi"), sem("wd_lo")
        hx_ready, hx_hi, hx_lo = sem("hx_ready"), sem("hx_hi"), sem("hx_lo")
        ss1_ready, ms1_ready, rstd1_ready = sem("ss1_ready"), sem("ms1_ready"), sem("rstd1_ready")
        tab_ready = sem("tab_ready")
        qkv_ready = sem("qkv_ready")
        rot_ready, qkv_used = sem("rot_ready"), sem("qkv_used")
        qk_ready, qkT_ready, kbd_ready, vbd_ready = sem("qk_ready"), sem("qkT_ready"), sem("kbd_ready"), sem("vbd_ready")
        scores_ready, top_ready, below_ready = sem("scores_ready"), sem("top_ready"), sem("below_ready")
        prob_ready, probT_ps, probT_ready = sem("prob_ready"), sem("probT_ps"), sem("probT_ready")
        ctx_ready, inv_ready, ctxn_ready, ctxT_ready = sem("ctx_ready"), sem("inv_ready"), sem("ctxn_ready"), sem("ctxT_ready")
        proj_ready, x2_ready = sem("proj_ready"), sem("x2_ready")
        ss2_ready, ms2_ready, rstd2_ready = sem("ss2_ready"), sem("ms2_ready"), sem("rstd2_ready")
        xn_ready, xnT_ps = sem("xn_ready"), sem("xnT_ps")
        h2_ready, h2_hi, h2_lo = sem("h2_ready"), sem("h2_hi"), sem("h2_lo")
        gu_ready, th_ready, sg_ready, hf_ready = sem("gu_ready"), sem("th_ready"), sem("sg_ready"), sem("hf_ready")
        hf_hi, hf_lo = sem("hf_hi"), sem("hf_lo")
        down_ready, final_ready = sem("down_ready"), sem("final_ready")

        out_v = out.rearrange("(t p) n -> p t n", p=P)
        block = ctx.enter_context(nc.Block())

        @block.sync
        def _(sp):
            sp.dma_start(pos_sb[:, :], pos).then_inc(in_pos, 16)
            sp.dma_start(pa[:, :], pack_a).then_inc(in_pa, 16)
            sp.dma_start(wqkv[:, :, :], w_qkv).then_inc(in_wqkv, 16)
            sp.dma_start(xk[:, 0:CT, :], x_tok[:, 0:CT]).then_inc(in_xk[0], 16)
            sp.dma_start(pb[:, :], pack_b).then_inc(in_pb, 16)
            sp.dma_start(wgu[:, 0:2, :], w_gu[:, 0:2]).then_inc(in_wgu[0], 16)
            for n in range(1, 4):
                sp.dma_start(wgu[:, 2 * n:2 * n + 2, :], w_gu[:, 2 * n:2 * n + 2]).then_inc(in_wgu[n], 16)
            sp.dma_start(xt[:, 1:GROUPS], xT[:, 1:GROUPS]).then_inc(in_xt[1], 16)
            for n in range(2):
                sp.dma_start(wd[:, 4 * n:4 * n + 4, :], w_d[:, 4 * n:4 * n + 4]).then_inc(in_wd[n], 16)
            sp.dma_start(xk[:, CT:TILES, :], x_tok[:, CT:TILES]).then_inc(in_xk[1], 16)
            for g in range(GROUPS - 1):
                sp.wait_ge(final_ready, g + 1)
                sp.dma_start(out_v[:, bass.ds(g * CT, CT), :], xk[:, bass.ds(g * CT, CT), :]).then_inc(out_done, 16)
            for c in range(CT):
                t = TILES - CT + c
                sp.wait_ge(final_ready, GROUPS + c)
                sp.dma_start(out_v[:, t, :], xk[:, t, :]).then_inc(out_done, 16)
            sp.wait_ge(out_done, 16 * (GROUPS - 1 + CT))

        def done(g, c, n):
            return g * CT + c + n

        def span(c, n, width):
            return slice(c * width, (c + n) * width)

        def bank_s(g, c, n):
            return ps_gu[:, 0].rearrange("p u t -> p (u t)") if (g, c) == (0, 1) else ps_s[:, :]

        def bank_t(g, c, n):
            return ps_gu[:, 1].rearrange("p u t -> p (u t)") if (g, c) == (0, 1) else ps_t[:, :]

        def sums(g, c):
            return ps_s[:, 0:HIDDEN] if g == GROUPS - 1 and c == 1 else ps_d[:, c, :]

        def split_products(pe, ps, lhs_h, lhs_l, rhs_h, rhs_l, first, last):
            pe.matmul(ps, lhs_h, rhs_h, start=first, stop=False)
            pe.matmul(ps, lhs_h, rhs_l, start=False, stop=False)
            return pe.matmul(ps, lhs_l, rhs_h, start=False, stop=last)

        @block.tensor
        def _(pe):
            def norm_scale(n):
                w, loaded, bank = ((tw1, in_pa, ps_s), (tw2, in_pb, ps_t))[n]
                pe.wait_ge(loaded, 16)
                for f in range(KH):
                    for k in range(KH):
                        mm = pe.matmul(bank[:, span(f, 1, BATCH)], w[:, k, span(f, 1, P)], cond[:, k, :],
                                       start=(k == 0), stop=(k == KH - 1))
                mm.then_inc(mod_ps, 1)

            def qkv(g, c0, n):
                if g == 0:
                    pe.wait_ge(wqkv_hi, 1)
                    pe.wait_ge(wqkv_lo, 1)
                else:
                    pe.wait_ge(ctxn_ready, CT * g)
                pe.wait_ge(hx_hi, done(g, c0, n))
                pe.wait_ge(hx_lo, done(g, c0, n))
                for c in range(c0, c0 + n):
                    for k in range(KH):
                        sl = span(c, 1, P)
                        mm = split_products(pe, ps_a[:, c, 0:QKV], hx_h[:, k, sl], hx_l[:, k, sl],
                                            wqkv_h[:, k, :], wqkv_l[:, k, :], k == 0, k == KH - 1)
                mm.then_inc(qkv_ready, n)

            def scores(g, c0, n):
                if g == 0:
                    pe.wait_ge(mod_ready, 1)
                else:
                    pe.wait_ge(x2_ready, CT * g)
                pe.wait_ge(kbd_ready, done(g, c0, n))
                for c in range(c0, c0 + n):
                    for j in range(HG):
                        mm = pe.matmul(bank_s(g, c0, n)[:, span(c * HG + j, 1, P)], qkT[:, c, span(j, 1, P)],
                                       kbd[:, c].rearrange("p b t -> p (b t)"), start=True, stop=True)
                mm.then_inc(scores_ready, n)

            def turn_probs(g, c, n):
                pe.wait_ge(prob_ready, done(g, c, n))
                if g:
                    pe.wait_ge(h2_ready, CT * g)
                else:
                    pe.wait_ge(mod_ready, 2)
                for i in range(c * HG, (c + n) * HG):
                    mm = pe.transpose(bank_t(g, c, n)[:, span(i, 1, P)], prob[:, span(i, 1, P)], ident)
                mm.then_inc(probT_ps, n)

            def context(g, c, n):
                pe.wait_ge(probT_ready, done(g, c, n))
                pe.wait_ge(vbd_ready, done(g, c, n))
                pe.wait_ge(ones_ready, 1)
                pe.wait_ge(rot_ready, done(g, c, n))
                for i in range(c * HG, (c + n) * HG):
                    mm = pe.matmul(ctx_ps[:, i, 0:VB + BPT], probT[:, span(i, 1, P)], vbd[:, i // HG, :],
                                   start=True, stop=True)
                mm.then_inc(ctx_ready, n)

            def project(g, c0, n):
                pe.wait_ge(ctxT_ready, done(g, c0, n))
                pe.wait_ge(below_ready, done(g, c0, n))
                for c in range(c0, c0 + n):
                    for j in range(HG):
                        mm = pe.matmul(bank_s(g, c0, n)[:, span(c, 1, HIDDEN)], ctxT[:, c * HG + j, :], wo[:, j, :],
                                       start=(j == 0), stop=(j == HG - 1))
                mm.then_inc(proj_ready, n)

            def turn_x(g, c0, n):
                pe.wait_ge(xn_ready, done(g, c0, n))
                pe.wait_ge(probT_ready, done(g, c0, n))
                for c in range(c0, c0 + n):
                    for k in range(KH):
                        mm = pe.transpose(bank_t(g, c0, n)[:, span(k * CT + c, 1, P)], xn[:, c, span(k, 1, P)], ident)
                mm.then_inc(xnT_ps, n)

            def gate_up(g, m):
                pe.wait_ge(h2_hi, CT * (g + 1))
                pe.wait_ge(h2_lo, CT * (g + 1))
                pe.wait_ge(wgu_hi, m // 2 + 1)
                pe.wait_ge(wgu_lo, m // 2 + 1)
                n = g * CHUNKS + m
                if n >= RING:
                    pe.wait_ge(hf_ready, n - RING + 1)
                for part in range(2):
                    for k in range(KH):
                        w = slice((part * KH + k) * P, (part * KH + k + 1) * P)
                        mm = split_products(pe, ps_gu[:, n % RING, part, :], wgu_h[:, m, w], wgu_l[:, m, w],
                                            h2_h[:, g, k, :], h2_l[:, g, k, :], k == 0, k == KH - 1)
                mm.then_inc(gu_ready, 1)

            def down(g, c, m0, m1):
                if m0 == 0 and c == 0 and g:
                    pe.wait_ge(final_ready, g)
                for m in range(m0, m1):
                    pe.wait_ge(wd_hi, m // 4 + 1)
                    pe.wait_ge(wd_lo, m // 4 + 1)
                    pe.wait_ge(hf_hi, g * CHUNKS + m + 1)
                    pe.wait_ge(hf_lo, g * CHUNKS + m + 1)
                    sl = slice(c * P, (c + 1) * P)
                    mm = split_products(pe, sums(g, c), hf_h[:, m, sl], hf_l[:, m, sl], wd_h[:, m, :], wd_l[:, m, :],
                                        m == 0, m == CHUNKS - 1)
                if m1 == CHUNKS:
                    mm.then_inc(down_ready, 1)

            norm_scale(0)
            for c in range(CT):
                qkv(0, c, 1)
            norm_scale(1)
            for stage in (scores, turn_probs, context, project):
                for c in range(CT):
                    stage(0, c, 1)
            qkv(1, 0, CT)
            for c in range(CT):
                turn_x(0, c, 1)
            for g in range(GROUPS - 1):
                a = g + 1
                for m in range(3):
                    gate_up(g, m)
                scores(a, 0, CT)
                for m in range(3, 6):
                    gate_up(g, m)
                turn_probs(a, 0, CT)
                gate_up(g, 6)
                context(a, 0, CT)
                gate_up(g, 7)
                down(g, 0, 0, 2)
                project(a, 0, CT)
                down(g, 0, 2, CHUNKS)
                if a + 1 < GROUPS:
                    qkv(a + 1, 0, CT)
                    turn_x(a, 0, CT)
                    down(g, 1, 0, CHUNKS)
                else:
                    down(g, 1, 0, 5)
                    turn_x(a, 0, CT)
                    down(g, 1, 5, CHUNKS)
            g = GROUPS - 1
            for m in range(CHUNKS):
                gate_up(g, m)
            down(g, 0, 0, CHUNKS - 1)
            down(g, 1, 0, 2)
            down(g, 0, CHUNKS - 1, CHUNKS)
            down(g, 1, 2, CHUNKS)

        @block.vector
        def _(dve):
            steps = [0]

            def link(ins):
                steps[0] += 1
                ins.then_inc(chain, 1)
                dve.wait_ge(chain, steps[0])

            dve.memset(half_neg[:, :], -0.5).then_inc(half_ready, 1)

            def modulation(n):
                dve.wait_ge(mod_ps, n + 1)
                bank = (ps_s, ps_t)[n]
                for f in range(KH):
                    ins = dve.tensor_scalar(mod[n][:, f, :], bank[:, f * BATCH:(f + 1) * BATCH], 1.0, ln[n][:, f:f + 1],
                                            ALU.add, ALU.mult)
                ins.then_inc(mod_ready, 1)
                dve.wait_ge(mod_ready, n + 1)

            def per_batch(m, g, c, n):
                return m[:, :, bass.ds(g * GB + c * BPT, n * BPT)].unsqueeze(3).broadcast_to([P, KH, n * BPT, SEQ])

            def by_batch(ap, c, n):
                return ap[:, :, span(c, n, P)].rearrange("p k (b s) -> p k b s", s=SEQ)

            def modulate_x(g, c, n):
                if g == 0:
                    dve.wait_ge(in_xt[0], 16)
                else:
                    dve.wait_ge(in_xt[1], 16)
                    dve.wait_ge(hx_hi, CT * g)
                dve.tensor_tensor(by_batch(hx, c, n), by_batch(xt[:, g], c, n), per_batch(mod[0], g, c, n),
                                  ALU.mult).then_inc(hx_ready, n)

            def low_x(g, c, n):
                dve.wait_ge(hx_hi, done(g, c, n))
                if g:
                    dve.wait_ge(qkv_ready, CT * g)
                sl = span(c, n, P)
                dve.tensor_tensor(hx_l[:, :, sl], hx[:, :, sl], hx_h[:, :, sl].bitcast(F32),
                                  ALU.subtract).then_inc(hx_lo, n)

            def mean_square_1(g):
                dve.wait_ge(ss1_ready, CT * (g + 1))
                dve.tensor_scalar(ms1[:, :], ss1[:, :], 1.0 / HIDDEN, EPS, ALU.mult, ALU.add).then_inc(ms1_ready, 1)

            def angles():
                dve.wait_ge(in_pos, 16)
                dve.wait_ge(in_small, 16)
                link(dve.tensor_tensor(ang[:, :, :], pos_sb[:, :].unsqueeze(2).broadcast_to([P, TILES, HALF]),
                                       freq.unsqueeze(1).broadcast_to([P, TILES, HALF]), ALU.mult))
                link(dve.tensor_scalar(redu[2][:, :, :], ang[:, :, :], 1.0 / TURN, ROUNDER, ALU.mult, ALU.add))
                link(dve.tensor_scalar(turns[:, :, :], redu[2][:, :, :], -ROUNDER, None, ALU.add))
                link(dve.scalar_tensor_tensor(out=redu[0][:, :, :], in0=turns[:, :, :], scalar=-TURN_1,
                                              in1=ang[:, :, :], op0=ALU.mult, op1=ALU.add))
                link(dve.scalar_tensor_tensor(out=redu[1][:, :, :], in0=turns[:, :, :], scalar=-TURN_2,
                                              in1=redu[0][:, :, :], op0=ALU.mult, op1=ALU.add))
                link(dve.tensor_scalar(sin_in[:, :, :], redu[1][:, :, :], PI_32, -PI_32, ALU.min, ALU.max))
                link(dve.scalar_tensor_tensor(out=redu[0][:, :, :], in0=sin_in[:, :, :], scalar=-1.0,
                                              in1=sin_in[:, :, :], op0=ALU.mult, op1=ALU.min))
                link(dve.tensor_scalar(cos_in[:, :, :], redu[0][:, :, :], TURN / 4, None, ALU.add))

            def tables(g):
                if g == 0:
                    dve.wait_ge(sin_ready, 3)
                else:
                    dve.wait_ge(vbd_ready, CT * g)
                dve.wait_ge(rstd1_ready, g + 1)
                r = rstd1[:, :]
                dve.tensor_tensor(cos_r[:, :, :, :],
                                  cos[:, bass.ds(g * CT, CT), :].unsqueeze(2).broadcast_to([P, CT, 2, HALF]),
                                  r.unsqueeze(2).unsqueeze(3).broadcast_to([P, CT, 2, HALF]), ALU.mult)
                dve.tensor_tensor(sin_r[:, :, :, :], sin[:, :, bass.ds(g * CT, CT), :],
                                  r.unsqueeze(1).unsqueeze(3).broadcast_to([P, 2, CT, HALF]), ALU.mult)
                dve.tensor_tensor(mask_r[:, :, :], mask.unsqueeze(1).broadcast_to([P, CT, BPT]),
                                  r.unsqueeze(2).broadcast_to([P, CT, BPT]), ALU.mult).then_inc(tab_ready, 1)

            def rotate_b(g, c, n):
                dve.wait_ge(tab_ready, g + 1)
                dve.wait_ge(qkv_ready, done(g, c, n))
                if g:
                    dve.wait_ge(qk_ready, CT * g)
                cs = slice(c, c + n)
                q = ps_a[:, cs, 0:QK].rearrange("p c (h d) -> p c h d", d=HD)
                b = rot_b[:, cs, :].rearrange("p c (h d) -> p c h d", d=HD)
                for half in range(2):
                    to, frm = span(half, 1, HALF), span(1 - half, 1, HALF)
                    dve.tensor_tensor(b[:, :, :, to], q[:, :, :, frm],
                                      sin_r[:, half, cs].unsqueeze(2).broadcast_to([P, n, HEADS + 1, HALF]), ALU.mult)

            def rotate_a(g, c, n):
                cs = slice(c, c + n)
                q = ps_a[:, cs, 0:QK].rearrange("p c (h d) -> p c h d", d=HD)
                a = rot_a[:, cs, :].rearrange("p c (h d) -> p c h d", d=HD)
                dve.tensor_tensor(a, q, cos_r[:, cs, :, :].rearrange("p c u d -> p c (u d)").unsqueeze(2)
                                  .broadcast_to([P, n, HEADS + 1, HD]), ALU.mult).then_inc(rot_ready, n)

            def add_rotation(g, c, n):
                cs = slice(c, c + n)
                dve.wait_ge(rot_ready, done(g, c, n))
                dve.tensor_tensor(qk_rot[:, cs, :], rot_a[:, cs, :], rot_b[:, cs, :], ALU.add).then_inc(qk_ready, n)

            def spread_v(g, c, n):
                if g:
                    dve.wait_ge(ctx_ready, CT * g)
                cs = slice(c, c + n)
                v = ps_a[:, cs, QK:QKV].unsqueeze(2).broadcast_to([P, n, BPT, HD])
                dve.tensor_tensor(vbd[:, cs, 0:VB].rearrange("p c (b d) -> p c b d", b=BPT), v,
                                  mask_r[:, cs, :].unsqueeze(3).broadcast_to([P, n, BPT, HD]),
                                  ALU.mult).then_inc(vbd_ready, n)

            def turn_qk(g, c, n):
                dve.wait_ge(qk_ready, done(g, c, n))
                if g:
                    dve.wait_ge(scores_ready, CT * g)
                cs = slice(c, c + n)
                dve.transpose(qkT[:, cs, :].rearrange("p c n -> p (c n)"),
                              qk_rot[:, cs, :].rearrange("p c n -> p (c n)")).then_inc(qkT_ready, n)

            def spread_k(g, c, n):
                dve.wait_ge(qkT_ready, done(g, c, n))
                cs = slice(c, c + n)
                dve.tensor_tensor(kbd[:, cs, :, :],
                                  qkT[:, cs, HEADS * HD:QK].unsqueeze(2).broadcast_to([P, n, BPT, SEQ]),
                                  mask.unsqueeze(1).unsqueeze(3).broadcast_to([P, n, BPT, SEQ]),
                                  ALU.mult).then_inc(kbd_ready, n)

            def by_row(ap):
                return ap.rearrange("p (n t) -> p n t", t=SEQ)

            def take_max(g, c, n):
                dve.wait_ge(scores_ready, done(g, c, n))
                s = by_row(bank_s(g, c, n)[:, span(c, n, HG * P)])
                t = top[:, span(c, n, HG * BPT)]
                dve.tensor_reduce(t, s, AX.X, ALU.max).then_inc(top_ready, n)

            def take_below(g, c, n):
                rows = n * HG * BPT
                s = by_row(bank_s(g, c, n)[:, span(c, n, HG * P)])
                t = top[:, span(c, n, HG * BPT)]
                dve.wait_ge(top_ready, done(g, c, n))
                if g:
                    dve.wait_ge(prob_ready, CT * g)
                dve.tensor_tensor(by_row(below[:, span(c, n, HG * P)]), s, t.unsqueeze(2).broadcast_to([P, rows, SEQ]),
                                  ALU.subtract).then_inc(below_ready, n)

            def invert(g, c, n):
                ns = span(c, n, HG)
                dve.wait_ge(ctx_ready, done(g, c, n))
                dve.reciprocal(inv[:, ns, :], ctx_ps[:, ns, VB:VB + BPT]).then_inc(inv_ready, n)

            def normalise(g, c, n):
                ns = span(c, n, HG)
                dve.wait_ge(inv_ready, done(g, c, n))
                dve.tensor_tensor(ctxn[:, span(c, n, HG * P)].rearrange("p (n b d) -> p n b d", b=BPT, d=HD),
                                  ctx_ps[:, ns, 0:VB].rearrange("p n (b d) -> p n b d", d=HD),
                                  inv[:, ns, :].unsqueeze(3).broadcast_to([P, n * HG, BPT, HD]),
                                  ALU.mult).then_inc(ctxn_ready, n)

            def turn_ctx(g, c, n):
                dve.wait_ge(ctxn_ready, done(g, c, n))
                if g:
                    dve.wait_ge(proj_ready, CT * g)
                dve.transpose(ctxT[:, span(c, n, HG), :].rearrange("p n t -> p (n t)"),
                              ctxn[:, span(c, n, HG * P)]).then_inc(ctxT_ready, n)

            def add_attention(g, c, n):
                dve.wait_ge(proj_ready, done(g, c, n))
                dve.wait_ge(ss1_ready, CT * (g + 1))
                x = xk[:, bass.ds(g * CT + c, n), :].rearrange("p c n -> p (c n)")
                dve.tensor_tensor(x, bank_s(g, c, n)[:, span(c, n, HIDDEN)], x, ALU.add).then_inc(x2_ready, n)

            def mean_square_2(g, c, n):
                dve.wait_ge(ss2_ready, done(g, c, n))
                dve.tensor_scalar(ms2[:, c:c + n], ss2[:, c:c + n], 1.0 / HIDDEN, EPS,
                                  ALU.mult, ALU.add).then_inc(ms2_ready, n)

            def scale_x(g, c0, n):
                dve.wait_ge(rstd2_ready, done(g, c0, n))
                if g:
                    dve.wait_ge(xnT_ps, CT * g)
                for c in range(c0, c0 + n):
                    ins = dve.tensor_scalar(xn[:, c, :], xk[:, g * CT + c, :], rstd2[:, c:c + 1], None, ALU.mult)
                ins.then_inc(xn_ready, n)

            def modulate_x2(g, c, n):
                dve.wait_ge(xnT_ps, done(g, c, n))
                if g:
                    dve.wait_ge(h2_hi, CT * g)
                t = bank_t(g, c, n).rearrange("p (k n) -> p k n", k=KH)
                dve.tensor_tensor(by_batch(h2, c, n), by_batch(t, c, n), per_batch(mod[1], g, c, n),
                                  ALU.mult).then_inc(h2_ready, n)

            def low_x2(g, c, n):
                sl = span(c, n, P)
                dve.wait_ge(h2_hi, done(g, c, n))
                dve.tensor_tensor(h2_l[:, g, :, sl], h2[:, :, sl], h2_h[:, g, :, sl].bitcast(F32),
                                  ALU.subtract).then_inc(h2_lo, n)

            def gated(g, m):
                n = g * CHUNKS + m
                dve.wait_ge(th_ready, n + 1)
                if n >= RING:
                    dve.wait_ge(hf_ready, n - RING + 1)
                dve.scalar_tensor_tensor(out=sg[:, n % RING], in0=th[:, n % RING], scalar=1.0,
                                         in1=ps_gu[:, n % RING, 0, :], op0=ALU.add, op1=ALU.mult).then_inc(sg_ready, 1)

            def hidden(g, m):
                n = g * CHUNKS + m
                dve.wait_ge(sg_ready, n + 1)
                if g:
                    dve.wait_ge(hf_lo, n - CHUNKS + 1)
                dve.tensor_tensor(hf[:, m], sg[:, n % RING], ps_gu[:, n % RING, 1, :], ALU.mult).then_inc(hf_ready, 1)

            def finish(g):
                dve.wait_ge(down_ready, CT * (g + 1))
                x = xk[:, bass.ds(g * CT, CT), :]
                dve.scalar_tensor_tensor(out=x, in0=ps_d[:, :, :], scalar=0.5, in1=x,
                                         op0=ALU.mult, op1=ALU.add).then_inc(final_ready, 1)

            def finish_last(c):
                t = TILES - CT + c
                dve.wait_ge(down_ready, t + 1)
                dve.scalar_tensor_tensor(out=xk[:, t, :], in0=sums(GROUPS - 1, c), scalar=0.5, in1=xk[:, t, :],
                                         op0=ALU.mult, op1=ALU.add).then_inc(final_ready, 1)

            angles()
            modulation(0)
            for c in range(CT):
                modulate_x(0, c, 1)
            dve.tensor_copy(vbd[:, :, VB:VB + BPT], mask.unsqueeze(1).broadcast_to([P, CT, BPT])).then_inc(ones_ready, 1)
            low_x(0, 0, 1)
            low_x(0, 1, 1)
            mean_square_1(0)
            tables(0)
            for stage in (rotate_b, rotate_a, add_rotation, turn_qk, spread_k, spread_v):
                stage(0, 0, 1)
            rotate_b(0, 1, 1)
            rotate_a(0, 1, 1)
            modulation(1)
            take_max(0, 0, 1)
            add_rotation(0, 1, 1)
            take_below(0, 0, 1)
            turn_qk(0, 1, 1)
            spread_k(0, 1, 1)
            spread_v(0, 1, 1)
            modulate_x(1, 0, CT)
            take_max(0, 1, 1)
            take_below(0, 1, 1)
            low_x(1, 0, CT)
            invert(0, 0, 1)
            normalise(0, 0, 1)
            turn_ctx(0, 0, 1)
            invert(0, 1, 1)
            normalise(0, 1, 1)
            turn_ctx(0, 1, 1)
            mean_square_1(1)
            for stages in ((add_attention,), (mean_square_2,), (scale_x,), (modulate_x2,), (low_x2,)):
                for c in range(CT):
                    for stage in stages:
                        stage(0, c, 1)
            tables(1)
            rotate_b(1, 0, CT)
            rotate_a(1, 0, CT)
            for g in range(GROUPS - 1):
                a, b = g + 1, g + 2
                add_rotation(a, 0, CT)
                turn_qk(a, 0, CT)
                spread_k(a, 0, CT)
                gated(g, 0)
                spread_v(a, 0, CT)
                hidden(g, 0)
                gated(g, 1)
                hidden(g, 1)
                gated(g, 2)
                hidden(g, 2)
                take_max(a, 0, CT)
                take_below(a, 0, CT)
                gated(g, 3)
                hidden(g, 3)
                gated(g, 4)
                hidden(g, 4)
                gated(g, 5)
                hidden(g, 5)
                if g:
                    finish(g - 1)
                gated(g, 6)
                hidden(g, 6)
                invert(a, 0, CT)
                normalise(a, 0, CT)
                turn_ctx(a, 0, CT)
                gated(g, 7)
                if b < GROUPS:
                    mean_square_1(b)
                hidden(g, 7)
                if b < GROUPS:
                    modulate_x(b, 0, CT)
                add_attention(a, 0, CT)
                if b < GROUPS:
                    low_x(b, 0, CT)
                mean_square_2(a, 0, CT)
                if b < GROUPS:
                    tables(b)
                scale_x(a, 0, CT)
                modulate_x2(a, 0, CT)
                if b < GROUPS:
                    rotate_b(b, 0, CT)
                low_x2(a, 0, CT)
                if b < GROUPS:
                    rotate_a(b, 0, CT)
            g = GROUPS - 1
            for m in range(CHUNKS):
                gated(g, m)
                hidden(g, m)
                if m == 0:
                    finish(g - 1)
            for c in range(CT):
                finish_last(c)

        @block.scalar
        def _(act):
            act.dma_start(small[:, :], pack_s).then_inc(in_small, 16)
            act.dma_start(xt[:, 0], xT[:, 0]).then_inc(in_xt[0], 16)

            def squares_1(g):
                if g == 0:
                    act.wait_ge(in_xk[0], 16)
                else:
                    act.wait_ge(in_xk[1], 16)
                    act.wait_ge(ms1_ready, g)
                for c in range(CT):
                    act.activation(sq1[:, c, :], xk[:, g * CT + c, :], ACT.Square,
                                   accum_out=ss1[:, c:c + 1]).then_inc(ss1_ready, 1)

            def squares_2(g, c0, n):
                act.wait_ge(x2_ready, done(g, c0, n))
                for c in range(c0, c0 + n):
                    act.activation(sq2[:, c, :], xk[:, g * CT + c, :], ACT.Square,
                                   accum_out=ss2[:, c:c + 1]).then_inc(ss2_ready, 1)

            def high_x(g, c, n):
                act.wait_ge(hx_ready, done(g, c, n))
                if g:
                    act.wait_ge(qkv_ready, CT * g)
                    act.wait_ge(hx_lo, CT * g)
                sl = span(c, n, P)
                act.activation(hx_h[:, :, sl], hx[:, :, sl], ACT.Copy).then_inc(hx_hi, n)

            def high_x2(g, c, n):
                act.wait_ge(h2_ready, done(g, c, n))
                sl = span(c, n, P)
                act.activation(h2_h[:, g, :, sl], h2[:, :, sl], ACT.Copy).then_inc(h2_hi, n)

            def exps(g, c, n):
                act.wait_ge(below_ready, done(g, c, n))
                if g:
                    act.wait_ge(probT_ps, CT * g)
                sl = span(c, n, HG * P)
                act.activation(prob[:, sl], below[:, sl], ACT.Exp, scale=float(HD) ** -0.5).then_inc(prob_ready, n)

            def copy_probT(g, c, n):
                act.wait_ge(probT_ps, done(g, c, n))
                if g:
                    act.wait_ge(ctx_ready, CT * g)
                sl = span(c, n, HG * P)
                act.activation(probT[:, sl], bank_t(g, c, n)[:, sl], ACT.Copy).then_inc(probT_ready, n)

            def tanh(g, m):
                n = g * CHUNKS + m
                act.wait_ge(gu_ready, n + 1)
                if n >= RING:
                    act.wait_ge(sg_ready, n - RING + 1)
                act.activation(th[:, n % RING], ps_gu[:, n % RING, 0, :], ACT.Tanh, scale=0.5).then_inc(th_ready, 1)

            def high_hidden(g, m):
                n = g * CHUNKS + m
                act.wait_ge(hf_ready, n + 1)
                if g:
                    act.wait_ge(down_ready, CT * g)
                act.activation(hf_h[:, m], hf[:, m], ACT.Copy).then_inc(hf_hi, 1)

            def high_gu(n):
                act.wait_ge(in_wgu[n], 16)
                act.activation(wgu_h[:, 2 * n:2 * n + 2, :], wgu[:, 2 * n:2 * n + 2, :], ACT.Copy).then_inc(wgu_hi, 1)

            act.wait_ge(chain, 6)
            for half, sign in enumerate((-1.0, 1.0)):
                act.activation(sin[:, half], sin_in[:, :, :], ACT.Sin, scale=sign).then_inc(sin_ready, 1)
            act.wait_ge(chain, 8)
            act.activation(cos[:, :, :], cos_in[:, :, :], ACT.Sin).then_inc(sin_ready, 1)
            act.wait_ge(in_wqkv, 16)
            act.activation(wqkv_h[:, :, :], wqkv[:, :, :], ACT.Copy).then_inc(wqkv_hi, 1)
            high_x(0, 0, 1)
            high_x(0, 1, 1)
            squares_1(0)
            high_gu(0)
            exps(0, 0, 1)
            high_x(1, 0, CT)
            exps(0, 1, 1)
            for c in range(CT):
                copy_probT(0, c, 1)
            squares_1(1)
            high_gu(1)
            squares_2(0, 0, 1)
            squares_2(0, 1, 1)
            high_gu(2)
            high_x2(0, 0, 1)
            high_x2(0, 1, 1)
            high_gu(3)
            for n in range(2):
                act.wait_ge(in_wd[n], 16)
                act.activation(wd_h[:, 4 * n:4 * n + 4, :], wd[:, 4 * n:4 * n + 4, :], ACT.Copy).then_inc(wd_hi, 1)
            for g in range(GROUPS - 1):
                a, b = g + 1, g + 2
                tanh(g, 0)
                tanh(g, 1)
                high_hidden(g, 0)
                tanh(g, 2)
                high_hidden(g, 1)
                high_hidden(g, 2)
                tanh(g, 3)
                exps(a, 0, CT)
                tanh(g, 4)
                high_hidden(g, 3)
                if b < GROUPS:
                    squares_1(b)
                tanh(g, 5)
                copy_probT(a, 0, CT)
                high_hidden(g, 4)
                tanh(g, 6)
                high_hidden(g, 5)
                tanh(g, 7)
                high_hidden(g, 6)
                high_hidden(g, 7)
                if b < GROUPS:
                    high_x(b, 0, CT)
                squares_2(a, 0, CT)
                high_x2(a, 0, CT)
            g = GROUPS - 1
            for m in range(CHUNKS):
                tanh(g, m)
                if m:
                    high_hidden(g, m - 1)
            high_hidden(g, CHUNKS - 1)

        @block.gpsimd
        def _(pool):
            def power_1(g):
                pool.wait_ge(ms1_ready, g + 1)
                if g:
                    pool.wait_ge(tab_ready, g)
                pool.tensor_tensor(rstd1[:, :], ms1[:, :], half_neg[:, :], ALU.pow).then_inc(rstd1_ready, 1)

            def power_2(g, c, n):
                pool.wait_ge(ms2_ready, done(g, c, n))
                if g:
                    pool.wait_ge(xn_ready, CT * g)
                pool.tensor_tensor(rstd2[:, c:c + n], ms2[:, c:c + n], half_neg[:, c:c + n],
                                   ALU.pow).then_inc(rstd2_ready, n)

            def low_hidden(g, m):
                n = g * CHUNKS + m
                pool.wait_ge(hf_hi, n + 1)
                pool.tensor_tensor(hf_l[:, m], hf[:, m], hf_h[:, m].bitcast(F32), ALU.subtract).then_inc(hf_lo, 1)

            def low_gu(n):
                sl = slice(2 * n, 2 * n + 2)
                pool.wait_ge(wgu_hi, n + 1)
                pool.tensor_tensor(wgu_l[:, sl, :], wgu[:, sl, :], wgu_h[:, sl, :].bitcast(F32),
                                   ALU.subtract).then_inc(wgu_lo, 1)

            pool.wait_ge(wqkv_hi, 1)
            pool.tensor_tensor(wqkv_l[:, :, :], wqkv[:, :, :], wqkv_h[:, :, :].bitcast(F32),
                               ALU.subtract).then_inc(wqkv_lo, 1)
            pool.wait_ge(half_ready, 1)
            power_1(0)
            low_gu(0)
            low_gu(1)
            power_1(1)
            power_2(0, 0, 1)
            power_2(0, 1, 1)
            low_gu(2)
            low_gu(3)
            for n in range(2):
                sl = slice(4 * n, 4 * n + 4)
                pool.wait_ge(wd_hi, n + 1)
                pool.tensor_tensor(wd_l[:, sl, :], wd[:, sl, :], wd_h[:, sl, :].bitcast(F32),
                                   ALU.subtract).then_inc(wd_lo, 1)
            for g in range(GROUPS - 1):
                a = g + 1
                for m in range(5):
                    low_hidden(g, m)
                if a + 1 < GROUPS:
                    power_1(a + 1)
                for m in range(5, CHUNKS):
                    low_hidden(g, m)
                power_2(a, 0, CT)
            for m in range(CHUNKS):
                low_hidden(GROUPS - 1, m)


def kernel(**inputs):
    import concourse.bacc as bacc
    from concourse.bass_utils import run_bass_kernel_spmd as run

    a = {n.replace("L0_cond_", ""): np.ascontiguousarray(v) for n, v in inputs.items()}

    def rows(w, parts):
        return w.reshape(parts, P, -1).transpose(1, 0, 2)

    x2d = a["x"].reshape(TOKENS, HIDDEN)
    xT = x2d.T.reshape(KH, P, GROUPS, GT).transpose(1, 2, 0, 3)
    x_tok = rows(x2d, TILES)
    pos = a["pos_BxS"].reshape(TILES, P).T
    batch_of = np.arange(P) // SEQ
    mask = (batch_of[:, None] == np.arange(BPT)[None, :]).astype(np.float32)
    exponent = np.arange(0, HD, 2, dtype=np.float32) / np.float32(HD)
    freq = np.broadcast_to(np.float32(1.0) / np.float32(ROPE_BASE) ** exponent, (P, HALF))
    pack_s = np.concatenate([a["ln1_w"].reshape(KH, P).T, a["ln2_w"].reshape(KH, P).T, mask, freq], axis=1)
    pack_a = np.concatenate([rows(a["cond_2048"].T, KH).reshape(P, -1), rows(a["ln1_tw"].T, KH).reshape(P, -1)], axis=1)
    w_qkv = rows(np.concatenate([a["Wq"], a["Wk"], a["Wv"]], axis=0).T, KH)
    pack_b = np.concatenate([np.eye(P, dtype=np.float32), rows(a["ln2_tw"].T, KH).reshape(P, -1),
                             rows(a["Wo"].T, HG).reshape(P, -1)], axis=1)
    w_gu = np.stack([a["Wg"], a["Wu"]]).reshape(2, CHUNKS, P, KH, P).transpose(4, 1, 0, 3, 2).reshape(P, CHUNKS, GU)
    w_d = rows(a["Wd"].T, CHUNKS)

    nc = bacc.Bacc("TRN2", target_bir_lowering=False, num_devices=1)
    arrays, args = {}, []
    for name, v in (("xT", xT), ("x_tok", x_tok), ("pos", pos), ("pack_s", pack_s), ("pack_a", pack_a), ("w_qkv", w_qkv),
                    ("pack_b", pack_b), ("w_gu", w_gu), ("w_d", w_d)):
        v = np.ascontiguousarray(v)
        arrays["in_" + name] = v
        args.append(nc.dram_tensor("in_" + name, v.shape, mybir.dt.from_np(v.dtype), kind="ExternalInput").ap())
    args.append(nc.dram_tensor("out_x", (TOKENS, HIDDEN), F32, kind="ExternalOutput").ap())
    block_program(nc, *args)
    r = run(nc, [arrays], core_ids=[0])
    return r.results[0]["out_x"].reshape(BATCH, SEQ, HIDDEN)
```

```python
from contextlib import ExitStack

import numpy as np
import concourse.bass as bass
from concourse import mybir

F32 = mybir.dt.float32
F32R = mybir.dt.float32r
I32 = mybir.dt.int32
ALU = mybir.AluOpType
ACT = mybir.ActivationFunctionType
AX = mybir.AxisListType

P = 128
BATCH, SEQ, HIDDEN = 32, 32, 256
HEADS, HD, INTER = 8, 32, 1024
TOKENS = BATCH * SEQ
HALF = HD // 2
KH = HIDDEN // P
QK = (HEADS + 1) * HD
QKV = QK + HD
BPT = P // SEQ
TILES = TOKENS // P
CT = 2
GROUPS = TILES // CT
GT = CT * P
GB = CT * BPT
HG = HEADS // BPT
CHUNKS = INTER // P
VB = BPT * HD
GU = 2 * KH * P
EPS = 1e-6
ROPE_BASE = 10000.0
RING = 3

A_COND, A_TW1 = 0, KH * BATCH
A_COLS = A_TW1 + KH * HIDDEN
S_LN1, S_LN2 = 0, KH
S_MASK = S_LN2 + KH
S_FREQ = S_MASK + BPT
S_COLS = S_FREQ + HALF
B_ID, B_TW2 = 0, P
B_WO = B_TW2 + KH * HIDDEN
B_COLS = B_WO + HG * HIDDEN

TURN = 2 * np.pi
TURN_1 = 6.28125
TURN_2 = float(np.float32(TURN - TURN_1))
ROUNDER = 1.5 * 2**23
PI_32 = 3.1415925


def block_program(nc, xT, x_tok, pos, pack_s, pack_a, w_qkv, pack_b, w_gu, w_d, out):
    with ExitStack() as ctx:
        def sb(name, shape, dt=F32):
            return ctx.enter_context(nc.sbuf_tensor(name, shape, dt))

        def sem(name):
            return ctx.enter_context(nc.semaphore(name))

        xt = sb("xt", [P, GROUPS, KH, GT])
        xk = sb("xk", [P, TILES, HIDDEN])
        pos_sb = sb("pos_sb", [P, TILES], I32)
        small = sb("small", [P, S_COLS])
        pa = sb("pa", [P, A_COLS])
        pb = sb("pb", [P, B_COLS])
        wqkv = sb("wqkv", [P, KH, QKV])
        wgu = sb("wgu", [P, CHUNKS, GU])
        wd = sb("wd", [P, CHUNKS, HIDDEN])
        cond = pa[:, A_COND:A_TW1].rearrange("p (k b) -> p k b", k=KH)
        tw1 = pa[:, A_TW1:A_COLS].rearrange("p (k n) -> p k n", k=KH)
        ln = [small[:, S_LN1:S_LN2], small[:, S_LN2:S_MASK]]
        mask = small[:, S_MASK:S_FREQ]
        freq = small[:, S_FREQ:S_COLS]
        ident = pb[:, B_ID:B_TW2]
        tw2 = pb[:, B_TW2:B_WO].rearrange("p (k n) -> p k n", k=KH)
        wo = pb[:, B_WO:B_COLS].rearrange("p (j n) -> p j n", j=HG)

        wqkv_h, wqkv_l = sb("wqkv_h", [P, KH, QKV], F32R), sb("wqkv_l", [P, KH, QKV], F32R)
        wgu_h, wgu_l = sb("wgu_h", [P, CHUNKS, GU], F32R), sb("wgu_l", [P, CHUNKS, GU], F32R)
        wd_h, wd_l = sb("wd_h", [P, CHUNKS, HIDDEN], F32R), sb("wd_l", [P, CHUNKS, HIDDEN], F32R)

        ang = sb("ang", [P, TILES, HALF])
        turns = sb("turns", [P, TILES, HALF])
        redu = [sb(f"redu{n}", [P, TILES, HALF]) for n in range(3)]
        sin_in = sb("sin_in", [P, TILES, HALF])
        cos_in = sb("cos_in", [P, TILES, HALF])
        cos = sb("cos", [P, TILES, HALF])
        sin = sb("sin", [P, 2, TILES, HALF])
        mod = [sb(f"mod{n}", [P, KH, BATCH]) for n in range(2)]
        half_neg = sb("half_neg", [P, CT])

        hx = sb("hx", [P, GROUPS, KH, GT])
        hx_h, hx_l = sb("hx_h", [P, GROUPS, KH, GT], F32R), sb("hx_l", [P, GROUPS, KH, GT], F32R)
        qkv_sb = sb("qkv_sb", [P, TILES, QKV])

        sq1, sq2 = sb("sq1", [P, CT, HIDDEN]), sb("sq2", [P, CT, HIDDEN])
        ss1, ms1, rstd1 = (sb(n, [P, CT]) for n in ("ss1", "ms1", "rstd1"))
        cos_r = sb("cos_r", [P, CT, 2, HALF])
        sin_r = sb("sin_r", [P, 2, CT, HALF])
        mask_r = sb("mask_r", [P, CT, BPT])
        rot_a = sb("rot_a", [P, CT, QK])
        rot_b = sb("rot_b", [P, CT, QK])
        qk_rot = sb("qk_rot", [P, CT, QK])
        qkT = sb("qkT", [P, CT, QK])
        kbd = sb("kbd", [P, CT, BPT, SEQ])
        vbd = sb("vbd", [P, CT, VB + BPT])
        top = sb("top", [P, CT * HG * BPT])
        below = sb("below", [P, CT * HG * P])
        prob = sb("prob", [P, CT * HG * P])
        probT = sb("probT", [P, CT * HG * P])
        inv = sb("inv", [P, CT * HG, BPT])
        ctxn = sb("ctxn", [P, CT * HG * P])
        ctxT = sb("ctxT", [P, CT * HG, P])
        ss2, ms2, rstd2 = (sb(n, [P, CT]) for n in ("ss2", "ms2", "rstd2"))
        xn = sb("xn", [P, CT, HIDDEN])
        h2 = sb("h2", [P, KH, GT])
        h2_h = sb("h2_h", [P, KH, GT], F32R)
        h2_l = sb("h2_l", [P, KH, GT], F32R)

        th = sb("th", [P, RING, GT])
        sg = sb("sg", [P, RING, GT])
        hf = sb("hf", [P, CHUNKS, GT])
        hf_h, hf_l = sb("hf_h", [P, CHUNKS, GT], F32R), sb("hf_l", [P, CHUNKS, GT], F32R)

        ps_a = ctx.enter_context(nc.psum_tensor("ps_a", [P, CT, 512], F32))
        ps_s = ctx.enter_context(nc.psum_tensor("ps_s", [P, 512], F32))
        ps_t = ctx.enter_context(nc.psum_tensor("ps_t", [P, 512], F32))
        ps_gu = ctx.enter_context(nc.psum_tensor("ps_gu", [P, RING, 2, GT], F32))
        ps_d = ctx.enter_context(nc.psum_tensor("ps_d", [P, CT, HIDDEN], F32))
        ctx_ps = ps_a[:, :, :].rearrange("p c (j n) -> p (c j) n", j=HG)

        in_small, in_pos, in_pa, in_wqkv, in_pb = (sem(n) for n in ("in_small", "in_pos", "in_pa", "in_wqkv", "in_pb"))
        in_xt = [sem(f"in_xt{n}") for n in range(3)]
        in_xk = [sem(f"in_xk{n}") for n in range(2)]
        in_wgu = [sem(f"in_wgu{n}") for n in range(4)]
        in_wd = [sem(f"in_wd{n}") for n in range(2)]
        out_done = sem("out_done")
        chain = sem("chain")
        half_ready = sem("half_ready")
        sin_ready = sem("sin_ready")
        mod_ps = sem("mod_ps")
        mod_ready = [sem(f"mod_ready{n}") for n in range(2)]
        ones_ready = sem("ones_ready")
        wqkv_hi, wqkv_lo = sem("wqkv_hi"), sem("wqkv_lo")
        wgu_hi, wgu_lo = sem("wgu_hi"), sem("wgu_lo")
        wd_hi, wd_lo = sem("wd_hi"), sem("wd_lo")
        hx_hi = sem("hx_hi")
        hx_ready = [sem(f"hx_ready{n}") for n in range(2)]
        hx_lo = [sem(f"hx_lo{n}") for n in range(2)]
        ss1_ready, ms1_ready, rstd1_ready = sem("ss1_ready"), sem("ms1_ready"), sem("rstd1_ready")
        tab_ready = sem("tab_ready")
        qkv_ready, qkv_copied = sem("qkv_ready"), sem("qkv_copied")
        rot_ready, qkv_used = sem("rot_ready"), sem("qkv_used")
        qk_ready, qkT_ready, kbd_ready, vbd_ready = sem("qk_ready"), sem("qkT_ready"), sem("kbd_ready"), sem("vbd_ready")
        scores_ready, top_ready, below_ready = sem("scores_ready"), sem("top_ready"), sem("below_ready")
        prob_ready, probT_ps, probT_ready = sem("prob_ready"), sem("probT_ps"), sem("probT_ready")
        ctx_ready, inv_ready, ctxn_ready, ctxT_ready = sem("ctx_ready"), sem("inv_ready"), sem("ctxn_ready"), sem("ctxT_ready")
        proj_ready, x2_ready = sem("proj_ready"), sem("x2_ready")
        ss2_ready, ms2_ready, rstd2_ready = sem("ss2_ready"), sem("ms2_ready"), sem("rstd2_ready")
        xn_ready, xnT_ps = sem("xn_ready"), sem("xnT_ps")
        h2_ready, h2_hi, h2_lo = sem("h2_ready"), sem("h2_hi"), sem("h2_lo")
        gu_ready, th_ready, sg_ready, hf_ready = sem("gu_ready"), sem("th_ready"), sem("sg_ready"), sem("hf_ready")
        hf_hi, hf_lo = sem("hf_hi"), sem("hf_lo")
        down_ready, final_ready = sem("down_ready"), sem("final_ready")

        out_v = out.rearrange("(t p) n -> p t n", p=P)
        block = ctx.enter_context(nc.Block())

        @block.sync
        def _(sp):
            sp.dma_start(pa[:, :], pack_a).then_inc(in_pa, 16)
            sp.dma_start(pos_sb[:, :], pos).then_inc(in_pos, 16)
            sp.dma_start(wqkv[:, :, :], w_qkv).then_inc(in_wqkv, 16)
            sp.dma_start(xk[:, 0:CT, :], x_tok[:, 0:CT]).then_inc(in_xk[0], 16)
            sp.dma_start(xt[:, 1], xT[:, 1]).then_inc(in_xt[1], 16)
            sp.dma_start(pb[:, :], pack_b).then_inc(in_pb, 16)
            sp.dma_start(xt[:, 2:GROUPS], xT[:, 2:GROUPS]).then_inc(in_xt[2], 16)
            sp.dma_start(wgu[:, 0:2, :], w_gu[:, 0:2]).then_inc(in_wgu[0], 16)
            sp.dma_start(wgu[:, 2:4, :], w_gu[:, 2:4]).then_inc(in_wgu[1], 16)
            sp.dma_start(xk[:, CT:TILES, :], x_tok[:, CT:TILES]).then_inc(in_xk[1], 16)
            for n in range(2, 4):
                sp.dma_start(wgu[:, 2 * n:2 * n + 2, :], w_gu[:, 2 * n:2 * n + 2]).then_inc(in_wgu[n], 16)
            for n in range(2):
                sp.dma_start(wd[:, 4 * n:4 * n + 4, :], w_d[:, 4 * n:4 * n + 4]).then_inc(in_wd[n], 16)
            for g in range(GROUPS - 1):
                sp.wait_ge(final_ready, CT * (g + 1))
                sp.dma_start(out_v[:, bass.ds(g * CT, CT), :], xk[:, bass.ds(g * CT, CT), :]).then_inc(out_done, 16)
            for c in range(CT):
                t = TILES - CT + c
                sp.wait_ge(final_ready, t + 1)
                sp.dma_start(out_v[:, t, :], xk[:, t, :]).then_inc(out_done, 16)
            sp.wait_ge(out_done, 16 * (GROUPS - 1 + CT))

        def done(g, c, n):
            return g * CT + c + n

        def span(c, n, width):
            return slice(c * width, (c + n) * width)

        def bank_s(g, c, n):
            return ps_gu[:, 0].rearrange("p u t -> p (u t)") if (g, c) == (0, 1) else ps_s[:, :]

        def bank_t(g, c, n):
            return ps_gu[:, 1].rearrange("p u t -> p (u t)") if (g, c) == (0, 1) else ps_t[:, :]

        def bank_p(g, c):
            if g:
                return (ps_s, ps_t)[c][:, 0:HIDDEN]
            return bank_s(g, c, 1)[:, span(c, 1, HIDDEN)]

        def bank_qkv(g, c):
            if g == 0:
                return ps_a[:, c, 0:QKV]
            return (ps_d[:, :, :].rearrange("p c n -> p (c n)"),
                    ps_gu[:, RING - 1].rearrange("p u t -> p (u t)"))[c][:, 0:QKV]

        sums = (ps_d[:, 0, :], ps_a[:, 1, 0:HIDDEN])

        def per_batch(m, g, c, n):
            return m[:, :, bass.ds(g * GB + c * BPT, n * BPT)].unsqueeze(3).broadcast_to([P, KH, n * BPT, SEQ])

        def by_batch(ap, c, n):
            return ap[:, :, span(c, n, P)].rearrange("p k (b s) -> p k b s", s=SEQ)

        def modulate_tiles(engine, g, c, n):
            return engine.tensor_tensor(by_batch(hx[:, g], c, n), by_batch(xt[:, g], c, n), per_batch(mod[0], g, c, n),
                                        ALU.mult)

        def low_tiles(engine, g, c, n):
            sl = span(c, n, P)
            return engine.tensor_tensor(hx_l[:, g, :, sl], hx[:, g, :, sl], hx_h[:, g, :, sl].bitcast(F32), ALU.subtract)

        def split_products(pe, ps, lhs_h, lhs_l, rhs_h, rhs_l, first, last):
            pe.matmul(ps, lhs_h, rhs_h, start=first, stop=False)
            pe.matmul(ps, lhs_h, rhs_l, start=False, stop=False)
            return pe.matmul(ps, lhs_l, rhs_h, start=False, stop=last)

        @block.tensor
        def _(pe):
            def norm_scale(n):
                w, loaded, bank = ((tw1, in_pa, ps_s), (tw2, in_pb, ps_t))[n]
                pe.wait_ge(loaded, 16)
                for f in range(KH):
                    for k in range(KH):
                        mm = pe.matmul(bank[:, span(f, 1, BATCH)], w[:, k, span(f, 1, P)], cond[:, k, :],
                                       start=(k == 0), stop=(k == KH - 1))
                mm.then_inc(mod_ps, 1)

            def qkv(g, c):
                if g > 1:
                    pe.wait_ge(qkv_copied, CT * (g - 2) + c + 1)
                maker, before = (0, 0) if g == 0 else (1, CT)
                pe.wait_ge(hx_hi, done(g, c, 1))
                for step, (x, w) in enumerate(((hx_h, wqkv_h), (hx_l, wqkv_h), (hx_h, wqkv_l))):
                    if step == 1:
                        pe.wait_ge(hx_lo[maker], done(g, c, 1) - before)
                    for k in range(KH):
                        if g == 0 and step == 0:
                            pe.wait_ge(wqkv_hi, k + 1)
                        if g == 0 and step == 2:
                            pe.wait_ge(wqkv_lo, k + 1)
                        mm = pe.matmul(bank_qkv(g, c), x[:, g, k, span(c, 1, P)], w[:, k, :],
                                       start=(step == 0 and k == 0), stop=(step == 2 and k == KH - 1))
                mm.then_inc(qkv_ready, 1)

            def scores(g, c0, n):
                if g == 0:
                    pe.wait_ge(mod_ready[0], 1)
                else:
                    pe.wait_ge(x2_ready, CT * g)
                pe.wait_ge(kbd_ready, done(g, c0, n))
                for c in range(c0, c0 + n):
                    for j in range(HG):
                        mm = pe.matmul(bank_s(g, c0, n)[:, span(c * HG + j, 1, P)], qkT[:, c, span(j, 1, P)],
                                       kbd[:, c].rearrange("p b t -> p (b t)"), start=True, stop=True)
                mm.then_inc(scores_ready, n)

            def turn_probs(g, c, n):
                pe.wait_ge(prob_ready, done(g, c, n))
                if g:
                    pe.wait_ge(h2_ready, CT * g)
                else:
                    pe.wait_ge(mod_ready[1], 1)
                for i in range(c * HG, (c + n) * HG):
                    mm = pe.transpose(bank_t(g, c, n)[:, span(i, 1, P)], prob[:, span(i, 1, P)], ident)
                mm.then_inc(probT_ps, n)

            def context(g, c, n):
                pe.wait_ge(probT_ready, done(g, c, n))
                pe.wait_ge(vbd_ready, done(g, c, n))
                pe.wait_ge(ones_ready, 1)
                if g:
                    pe.wait_ge(ctxn_ready, CT * g)
                if g > 1:
                    pe.wait_ge(final_ready, CT * (g - 1))
                else:
                    pe.wait_ge(rot_ready, done(g, c, n))
                for i in range(c * HG, (c + n) * HG):
                    mm = pe.matmul(ctx_ps[:, i, 0:VB + BPT], probT[:, span(i, 1, P)], vbd[:, i // HG, :],
                                   start=True, stop=True)
                mm.then_inc(ctx_ready, n)

            def project(g, c0, n):
                pe.wait_ge(ctxT_ready, done(g, c0, n))
                pe.wait_ge(below_ready, done(g, c0, n))
                pe.wait_ge(probT_ready, done(g, c0, n))
                for c in range(c0, c0 + n):
                    for j in range(HG):
                        mm = pe.matmul(bank_p(g, c), ctxT[:, c * HG + j, :], wo[:, j, :],
                                       start=(j == 0), stop=(j == HG - 1))
                    mm.then_inc(proj_ready, 1)

            def turn_x(g, c0, n):
                pe.wait_ge(xn_ready, done(g, c0, n))
                pe.wait_ge(x2_ready, done(g, c0, n))
                for c in range(c0, c0 + n):
                    for k in range(KH):
                        mm = pe.transpose(bank_t(g, c0, n)[:, span(k * CT + c, 1, P)], xn[:, c, span(k, 1, P)], ident)
                mm.then_inc(xnT_ps, n)

            def gate_up(g, m):
                pe.wait_ge(h2_hi, CT * (g + 1))
                if g == 0:
                    pe.wait_ge(wgu_hi, m // 2 + 1)
                    pe.wait_ge(wgu_lo, m // 2 + 1)
                n = g * CHUNKS + m
                if n == RING - 1:
                    pe.wait_ge(qkv_copied, TILES - CT)
                if n >= RING:
                    pe.wait_ge(hf_ready, n - RING + 1)
                for part in range(2):
                    for step, (w, h) in enumerate(((wgu_h, h2_h), (wgu_l, h2_h), (wgu_h, h2_l))):
                        if part == 0 and step == 2 and m == 0:
                            pe.wait_ge(h2_lo, CT * (g + 1))
                        for k in range(KH):
                            mm = pe.matmul(ps_gu[:, n % RING, part, :], w[:, m, span(part * KH + k, 1, P)], h[:, k, :],
                                           start=(step == 0 and k == 0), stop=(step == 2 and k == KH - 1))
                mm.then_inc(gu_ready, 1)

            def down(g, c, m0, m1):
                if m0 == 0 and c == 0 and g:
                    pe.wait_ge(final_ready, CT * g)
                for m in range(m0, m1):
                    pe.wait_ge(wd_hi, m // 4 + 1)
                    pe.wait_ge(wd_lo, m // 4 + 1)
                    pe.wait_ge(hf_hi, g * CHUNKS + m + 1)
                    pe.wait_ge(hf_lo, g * CHUNKS + m + 1)
                    sl = slice(c * P, (c + 1) * P)
                    mm = split_products(pe, sums[c], hf_h[:, m, sl], hf_l[:, m, sl], wd_h[:, m, :], wd_l[:, m, :],
                                        m == 0, m == CHUNKS - 1)
                if m1 == CHUNKS:
                    mm.then_inc(down_ready, 1)

            norm_scale(0)
            qkv(0, 0)
            qkv(0, 1)
            norm_scale(1)
            scores(0, 0, 1)
            qkv(1, 0)
            turn_probs(0, 0, 1)
            scores(0, 1, 1)
            context(0, 0, 1)
            qkv(1, 1)
            turn_probs(0, 1, 1)
            context(0, 1, 1)
            project(0, 0, 1)
            qkv(2, 0)
            project(0, 1, 1)
            qkv(2, 1)
            turn_x(0, 0, 1)
            qkv(3, 0)
            turn_x(0, 1, 1)
            qkv(3, 1)
            for g in range(GROUPS - 1):
                a = g + 1
                gate_up(g, 0)
                gate_up(g, 1)
                scores(a, 0, CT)
                for m in range(2, 5):
                    gate_up(g, m)
                turn_probs(a, 0, CT)
                gate_up(g, 5)
                context(a, 0, CT)
                gate_up(g, 6)
                down(g, 0, 0, 4)
                project(a, 0, CT)
                gate_up(g, 7)
                down(g, 0, 4, 7)
                down(g, 1, 0, 3)
                turn_x(a, 0, CT)
                down(g, 1, 3, 7)
                down(g, 0, 7, CHUNKS)
                down(g, 1, 7, CHUNKS)
            g = GROUPS - 1
            for m in range(CHUNKS):
                gate_up(g, m)
            down(g, 0, 0, CHUNKS - 1)
            down(g, 1, 0, 2)
            down(g, 0, CHUNKS - 1, CHUNKS)
            down(g, 1, 2, CHUNKS)

        @block.vector
        def _(dve):
            steps = [0]

            def link(ins):
                steps[0] += 1
                ins.then_inc(chain, 1)
                dve.wait_ge(chain, steps[0])

            dve.memset(half_neg[:, :], -0.5).then_inc(half_ready, 1)

            def modulation():
                dve.wait_ge(mod_ps, 1)
                for f in range(KH):
                    ins = dve.tensor_scalar(mod[0][:, f, :], ps_s[:, span(f, 1, BATCH)], 1.0, ln[0][:, f:f + 1],
                                            ALU.add, ALU.mult)
                ins.then_inc(mod_ready[0], 1)
                dve.wait_ge(mod_ready[0], 1)

            def modulate_x(c):
                dve.wait_ge(in_xt[0], 16)
                modulate_tiles(dve, 0, c, 1).then_inc(hx_ready[0], 1)

            def low_x(c):
                dve.wait_ge(hx_hi, c + 1)
                low_tiles(dve, 0, c, 1).then_inc(hx_lo[0], 1)

            def mean_square_1(g):
                dve.wait_ge(ss1_ready, CT * (g + 1))
                dve.tensor_scalar(ms1[:, :], ss1[:, :], 1.0 / HIDDEN, EPS, ALU.mult, ALU.add).then_inc(ms1_ready, 1)

            def angles(last):
                if last:
                    link(dve.scalar_tensor_tensor(out=redu[0][:, :, :], in0=sin_in[:, :, :], scalar=-1.0,
                                                  in1=sin_in[:, :, :], op0=ALU.mult, op1=ALU.min))
                    dve.tensor_scalar(cos_in[:, :, :], redu[0][:, :, :], TURN / 4, None, ALU.add).then_inc(chain, 1)
                    return
                dve.wait_ge(in_pos, 16)
                dve.wait_ge(in_small, 16)
                link(dve.tensor_tensor(ang[:, :, :], pos_sb[:, :].unsqueeze(2).broadcast_to([P, TILES, HALF]),
                                       freq.unsqueeze(1).broadcast_to([P, TILES, HALF]), ALU.mult))
                link(dve.tensor_scalar(redu[2][:, :, :], ang[:, :, :], 1.0 / TURN, ROUNDER, ALU.mult, ALU.add))
                link(dve.tensor_scalar(turns[:, :, :], redu[2][:, :, :], -ROUNDER, None, ALU.add))
                link(dve.scalar_tensor_tensor(out=redu[0][:, :, :], in0=turns[:, :, :], scalar=-TURN_1,
                                              in1=ang[:, :, :], op0=ALU.mult, op1=ALU.add))
                link(dve.scalar_tensor_tensor(out=redu[1][:, :, :], in0=turns[:, :, :], scalar=-TURN_2,
                                              in1=redu[0][:, :, :], op0=ALU.mult, op1=ALU.add))
                link(dve.tensor_scalar(sin_in[:, :, :], redu[1][:, :, :], PI_32, -PI_32, ALU.min, ALU.max))

            def tables(g):
                if g == 0:
                    dve.wait_ge(sin_ready, 3)
                else:
                    dve.wait_ge(vbd_ready, CT * g)
                dve.wait_ge(rstd1_ready, g + 1)
                r = rstd1[:, :]
                dve.tensor_tensor(cos_r[:, :, :, :],
                                  cos[:, bass.ds(g * CT, CT), :].unsqueeze(2).broadcast_to([P, CT, 2, HALF]),
                                  r.unsqueeze(2).unsqueeze(3).broadcast_to([P, CT, 2, HALF]), ALU.mult)
                dve.tensor_tensor(sin_r[:, :, :, :], sin[:, :, bass.ds(g * CT, CT), :],
                                  r.unsqueeze(1).unsqueeze(3).broadcast_to([P, 2, CT, HALF]), ALU.mult)
                dve.tensor_tensor(mask_r[:, :, :], mask.unsqueeze(1).broadcast_to([P, CT, BPT]),
                                  r.unsqueeze(2).broadcast_to([P, CT, BPT]), ALU.mult).then_inc(tab_ready, 1)

            def raw(g, cs):
                return qkv_sb[:, g * CT + cs.start:g * CT + cs.stop, :] if g else ps_a[:, cs, :]

            def rotate_b(g, c, n):
                dve.wait_ge(tab_ready, g + 1)
                if g:
                    dve.wait_ge(qkv_copied, CT * g)
                else:
                    dve.wait_ge(qkv_ready, c + n)
                if g:
                    dve.wait_ge(qk_ready, CT * g)
                cs = slice(c, c + n)
                q = raw(g, cs)[:, :, 0:QK].rearrange("p c (h d) -> p c h d", d=HD)
                b = rot_b[:, cs, :].rearrange("p c (h d) -> p c h d", d=HD)
                for half in range(2):
                    to, frm = span(half, 1, HALF), span(1 - half, 1, HALF)
                    dve.tensor_tensor(b[:, :, :, to], q[:, :, :, frm],
                                      sin_r[:, half, cs].unsqueeze(2).broadcast_to([P, n, HEADS + 1, HALF]), ALU.mult)

            def rotate_a(g, c, n):
                cs = slice(c, c + n)
                q = raw(g, cs)[:, :, 0:QK].rearrange("p c (h d) -> p c h d", d=HD)
                a = rot_a[:, cs, :].rearrange("p c (h d) -> p c h d", d=HD)
                dve.tensor_tensor(a, q, cos_r[:, cs, :, :].rearrange("p c u d -> p c (u d)").unsqueeze(2)
                                  .broadcast_to([P, n, HEADS + 1, HD]), ALU.mult).then_inc(rot_ready, n)

            def add_rotation(g, c, n):
                cs = slice(c, c + n)
                dve.wait_ge(rot_ready, done(g, c, n))
                dve.tensor_tensor(qk_rot[:, cs, :], rot_a[:, cs, :], rot_b[:, cs, :], ALU.add).then_inc(qk_ready, n)

            def spread_v(g, c, n):
                if g:
                    dve.wait_ge(ctx_ready, CT * g)
                cs = slice(c, c + n)
                v = raw(g, cs)[:, :, QK:QKV].unsqueeze(2).broadcast_to([P, n, BPT, HD])
                dve.tensor_tensor(vbd[:, cs, 0:VB].rearrange("p c (b d) -> p c b d", b=BPT), v,
                                  mask_r[:, cs, :].unsqueeze(3).broadcast_to([P, n, BPT, HD]),
                                  ALU.mult).then_inc(vbd_ready, n)

            def turn_qk(g, c, n):
                dve.wait_ge(qk_ready, done(g, c, n))
                if g:
                    dve.wait_ge(scores_ready, CT * g)
                cs = slice(c, c + n)
                dve.transpose(qkT[:, cs, :].rearrange("p c n -> p (c n)"),
                              qk_rot[:, cs, :].rearrange("p c n -> p (c n)")).then_inc(qkT_ready, n)

            def spread_k(g, c, n):
                dve.wait_ge(qkT_ready, done(g, c, n))
                cs = slice(c, c + n)
                dve.tensor_tensor(kbd[:, cs, :, :],
                                  qkT[:, cs, HEADS * HD:QK].unsqueeze(2).broadcast_to([P, n, BPT, SEQ]),
                                  mask.unsqueeze(1).unsqueeze(3).broadcast_to([P, n, BPT, SEQ]),
                                  ALU.mult).then_inc(kbd_ready, n)

            def by_row(ap):
                return ap.rearrange("p (n t) -> p n t", t=SEQ)

            def take_max(g, c, n):
                dve.wait_ge(scores_ready, done(g, c, n))
                s = by_row(bank_s(g, c, n)[:, span(c, n, HG * P)])
                t = top[:, span(c, n, HG * BPT)]
                dve.tensor_reduce(t, s, AX.X, ALU.max).then_inc(top_ready, n)

            def take_below(g, c, n):
                rows = n * HG * BPT
                s = by_row(bank_s(g, c, n)[:, span(c, n, HG * P)])
                t = top[:, span(c, n, HG * BPT)]
                dve.wait_ge(top_ready, done(g, c, n))
                if g:
                    dve.wait_ge(prob_ready, CT * g)
                dve.tensor_tensor(by_row(below[:, span(c, n, HG * P)]), s, t.unsqueeze(2).broadcast_to([P, rows, SEQ]),
                                  ALU.subtract).then_inc(below_ready, n)

            def invert(g, c, n):
                ns = span(c, n, HG)
                dve.wait_ge(ctx_ready, done(g, c, n))
                dve.reciprocal(inv[:, ns, :], ctx_ps[:, ns, VB:VB + BPT]).then_inc(inv_ready, n)

            def normalise(g, c, n):
                ns = span(c, n, HG)
                dve.wait_ge(inv_ready, done(g, c, n))
                dve.tensor_tensor(ctxn[:, span(c, n, HG * P)].rearrange("p (n b d) -> p n b d", b=BPT, d=HD),
                                  ctx_ps[:, ns, 0:VB].rearrange("p n (b d) -> p n b d", d=HD),
                                  inv[:, ns, :].unsqueeze(3).broadcast_to([P, n * HG, BPT, HD]),
                                  ALU.mult).then_inc(ctxn_ready, n)

            def turn_ctx(g, c, n):
                dve.wait_ge(ctxn_ready, done(g, c, n))
                if g:
                    dve.wait_ge(proj_ready, CT * g)
                dve.transpose(ctxT[:, span(c, n, HG), :].rearrange("p n t -> p (n t)"),
                              ctxn[:, span(c, n, HG * P)]).then_inc(ctxT_ready, n)

            def add_attention(g, c, n):
                dve.wait_ge(proj_ready, done(g, c, n))
                dve.wait_ge(ss1_ready, CT * (g + 1))
                x = xk[:, bass.ds(g * CT + c, n), :].rearrange("p c n -> p (c n)")
                dve.tensor_tensor(x, bank_p(g, c), x, ALU.add).then_inc(x2_ready, n)

            def mean_square_2(g, c, n):
                dve.wait_ge(ss2_ready, done(g, c, n))
                dve.tensor_scalar(ms2[:, c:c + n], ss2[:, c:c + n], 1.0 / HIDDEN, EPS,
                                  ALU.mult, ALU.add).then_inc(ms2_ready, n)

            def scale_x(g, c0, n):
                dve.wait_ge(rstd2_ready, done(g, c0, n))
                if g:
                    dve.wait_ge(xnT_ps, CT * g)
                for c in range(c0, c0 + n):
                    ins = dve.tensor_scalar(xn[:, c, :], xk[:, g * CT + c, :], rstd2[:, c:c + 1], None, ALU.mult)
                ins.then_inc(xn_ready, n)

            def modulate_x2(g, c, n):
                dve.wait_ge(xnT_ps, done(g, c, n))
                if g == 0:
                    dve.wait_ge(mod_ready[1], 1)
                if g:
                    dve.wait_ge(h2_hi, CT * g)
                t = bank_t(g, c, n).rearrange("p (k n) -> p k n", k=KH)
                dve.tensor_tensor(by_batch(h2, c, n), by_batch(t, c, n), per_batch(mod[1], g, c, n),
                                  ALU.mult).then_inc(h2_ready, n)

            def low_x2(g, c, n):
                sl = span(c, n, P)
                dve.wait_ge(h2_hi, done(g, c, n))
                dve.tensor_tensor(h2_l[:, :, sl], h2[:, :, sl], h2_h[:, :, sl].bitcast(F32),
                                  ALU.subtract).then_inc(h2_lo, n)

            def gated(g, m):
                n = g * CHUNKS + m
                dve.wait_ge(th_ready, n + 1)
                if n >= RING:
                    dve.wait_ge(hf_ready, n - RING + 1)
                dve.scalar_tensor_tensor(out=sg[:, n % RING], in0=th[:, n % RING], scalar=1.0,
                                         in1=ps_gu[:, n % RING, 0, :], op0=ALU.add, op1=ALU.mult).then_inc(sg_ready, 1)

            def hidden(g, m):
                n = g * CHUNKS + m
                dve.wait_ge(sg_ready, n + 1)
                if g:
                    dve.wait_ge(hf_lo, n - CHUNKS + 1)
                dve.tensor_tensor(hf[:, m], sg[:, n % RING], ps_gu[:, n % RING, 1, :], ALU.mult).then_inc(hf_ready, 1)

            def finish(g, c):
                t = g * CT + c
                dve.wait_ge(down_ready, t + 1)
                dve.scalar_tensor_tensor(out=xk[:, t, :], in0=sums[c], scalar=0.5, in1=xk[:, t, :],
                                         op0=ALU.mult, op1=ALU.add).then_inc(final_ready, 1)

            angles(False)
            modulation()
            for c in range(CT):
                modulate_x(c)
            dve.tensor_copy(vbd[:, :, VB:VB + BPT], mask.unsqueeze(1).broadcast_to([P, CT, BPT])).then_inc(ones_ready, 1)
            low_x(0)
            angles(True)
            mean_square_1(0)
            low_x(1)
            tables(0)
            for stage in (rotate_b, rotate_a, add_rotation, turn_qk, spread_k):
                stage(0, 0, 1)
            rotate_b(0, 1, 1)
            rotate_a(0, 1, 1)
            take_max(0, 0, 1)
            take_below(0, 0, 1)
            add_rotation(0, 1, 1)
            turn_qk(0, 1, 1)
            spread_v(0, 0, 1)
            spread_k(0, 1, 1)
            spread_v(0, 1, 1)
            take_max(0, 1, 1)
            invert(0, 0, 1)
            take_below(0, 1, 1)
            normalise(0, 0, 1)
            turn_ctx(0, 0, 1)
            invert(0, 1, 1)
            mean_square_1(1)
            normalise(0, 1, 1)
            turn_ctx(0, 1, 1)
            add_attention(0, 0, 1)
            tables(1)
            mean_square_2(0, 0, 1)
            rotate_b(1, 0, 1)
            add_attention(0, 1, 1)
            scale_x(0, 0, 1)
            rotate_b(1, 1, 1)
            mean_square_2(0, 1, 1)
            modulate_x2(0, 0, 1)
            scale_x(0, 1, 1)
            rotate_a(1, 0, 1)
            low_x2(0, 0, 1)
            modulate_x2(0, 1, 1)
            add_rotation(1, 0, 1)
            low_x2(0, 1, 1)
            rotate_a(1, 1, 1)
            turn_qk(1, 0, 1)
            add_rotation(1, 1, 1)
            spread_k(1, 0, 1)
            turn_qk(1, 1, 1)
            spread_k(1, 1, 1)
            for g in range(GROUPS - 1):
                a, b = g + 1, g + 2
                gated(g, 0)
                spread_v(a, 0, CT)
                hidden(g, 0)
                gated(g, 1)
                hidden(g, 1)
                take_max(a, 0, CT)
                take_below(a, 0, CT)
                gated(g, 2)
                hidden(g, 2)
                if g:
                    for c in range(CT):
                        finish(g - 1, c)
                gated(g, 3)
                hidden(g, 3)
                if b < GROUPS:
                    mean_square_1(b)
                gated(g, 4)
                hidden(g, 4)
                gated(g, 5)
                hidden(g, 5)
                invert(a, 0, CT)
                normalise(a, 0, CT)
                turn_ctx(a, 0, CT)
                if b < GROUPS:
                    tables(b)
                    rotate_b(b, 0, CT)
                gated(g, 6)
                add_attention(a, 0, 1)
                hidden(g, 6)
                add_attention(a, 1, 1)
                if b < GROUPS:
                    rotate_a(b, 0, CT)
                mean_square_2(a, 0, CT)
                gated(g, 7)
                for c in range(CT):
                    scale_x(a, c, 1)
                hidden(g, 7)
                modulate_x2(a, 0, 1)
                modulate_x2(a, 1, 1)
                low_x2(a, 0, 1)
                low_x2(a, 1, 1)
                if b < GROUPS:
                    add_rotation(b, 0, CT)
                    turn_qk(b, 0, CT)
                    spread_k(b, 0, CT)
            g = GROUPS - 1
            for m in range(CHUNKS):
                gated(g, m)
                hidden(g, m)
                if m == 0:
                    for c in range(CT):
                        finish(g - 1, c)
            for c in range(CT):
                finish(g, c)

        @block.scalar
        def _(act):
            act.dma_start(small[:, :], pack_s).then_inc(in_small, 16)
            act.dma_start(xt[:, 0], xT[:, 0]).then_inc(in_xt[0], 16)

            def squares_1(g):
                if g == 0:
                    act.wait_ge(in_xk[0], 16)
                else:
                    act.wait_ge(in_xk[1], 16)
                    act.wait_ge(ms1_ready, g)
                for c in range(CT):
                    act.activation(sq1[:, c, :], xk[:, g * CT + c, :], ACT.Square,
                                   accum_out=ss1[:, c:c + 1]).then_inc(ss1_ready, 1)

            def squares_2(g, c0, n):
                act.wait_ge(x2_ready, done(g, c0, n))
                for c in range(c0, c0 + n):
                    act.activation(sq2[:, c, :], xk[:, g * CT + c, :], ACT.Square,
                                   accum_out=ss2[:, c:c + 1]).then_inc(ss2_ready, 1)

            def high_x(g, c, n):
                if g:
                    act.wait_ge(hx_ready[1], done(g, c, n) - CT)
                else:
                    act.wait_ge(hx_ready[0], c + n)
                sl = span(c, n, P)
                act.activation(hx_h[:, g, :, sl], hx[:, g, :, sl], ACT.Copy).then_inc(hx_hi, n)

            def modulation():
                act.wait_ge(mod_ps, 2)
                act.wait_ge(in_small, 16)
                for f in range(KH):
                    ins = act.activation(mod[1][:, f, :], ps_t[:, span(f, 1, BATCH)], ACT.Identity,
                                         bias=ln[1][:, f:f + 1], scale=ln[1][:, f:f + 1])
                ins.then_inc(mod_ready[1], 1)

            def copy_qkv(g, c):
                act.wait_ge(qkv_ready, done(g, c, 1))
                act.activation(qkv_sb[:, g * CT + c, :], bank_qkv(g, c), ACT.Copy).then_inc(qkv_copied, 1)

            def high_x2(g, c, n):
                act.wait_ge(h2_ready, done(g, c, n))
                if g:
                    act.wait_ge(gu_ready, CHUNKS * g)
                sl = span(c, n, P)
                act.activation(h2_h[:, :, sl], h2[:, :, sl], ACT.Copy).then_inc(h2_hi, n)

            def exps(g, c, n):
                act.wait_ge(below_ready, done(g, c, n))
                if g:
                    act.wait_ge(probT_ps, CT * g)
                sl = span(c, n, HG * P)
                act.activation(prob[:, sl], below[:, sl], ACT.Exp, scale=float(HD) ** -0.5).then_inc(prob_ready, n)

            def copy_probT(g, c, n):
                act.wait_ge(probT_ps, done(g, c, n))
                if g:
                    act.wait_ge(ctx_ready, CT * g)
                sl = span(c, n, HG * P)
                act.activation(probT[:, sl], bank_t(g, c, n)[:, sl], ACT.Copy).then_inc(probT_ready, n)

            def tanh(g, m):
                n = g * CHUNKS + m
                act.wait_ge(gu_ready, n + 1)
                if n >= RING:
                    act.wait_ge(sg_ready, n - RING + 1)
                act.activation(th[:, n % RING], ps_gu[:, n % RING, 0, :], ACT.Tanh, scale=0.5).then_inc(th_ready, 1)

            def high_hidden(g, m):
                n = g * CHUNKS + m
                act.wait_ge(hf_ready, n + 1)
                if g:
                    act.wait_ge(down_ready, CT * g)
                act.activation(hf_h[:, m], hf[:, m], ACT.Copy).then_inc(hf_hi, 1)

            def high_gu(n):
                act.wait_ge(in_wgu[n], 16)
                act.activation(wgu_h[:, 2 * n:2 * n + 2, :], wgu[:, 2 * n:2 * n + 2, :], ACT.Copy).then_inc(wgu_hi, 1)

            def high_down(n):
                act.wait_ge(in_wd[n], 16)
                act.activation(wd_h[:, 4 * n:4 * n + 4, :], wd[:, 4 * n:4 * n + 4, :], ACT.Copy).then_inc(wd_hi, 1)

            act.wait_ge(chain, 6)
            for half, sign in enumerate((-1.0, 1.0)):
                act.activation(sin[:, half], sin_in[:, :, :], ACT.Sin, scale=sign).then_inc(sin_ready, 1)
            act.wait_ge(in_wqkv, 16)
            act.activation(wqkv_h[:, 0, :], wqkv[:, 0, :], ACT.Copy).then_inc(wqkv_hi, 1)
            high_x(0, 0, 1)
            act.activation(wqkv_h[:, 1, :], wqkv[:, 1, :], ACT.Copy).then_inc(wqkv_hi, 1)
            squares_1(0)
            high_x(0, 1, 1)
            act.wait_ge(chain, 8)
            act.activation(cos[:, :, :], cos_in[:, :, :], ACT.Sin).then_inc(sin_ready, 1)
            high_x(1, 0, CT)
            modulation()
            high_x(2, 0, CT)
            exps(0, 0, 1)
            copy_qkv(1, 0)
            copy_probT(0, 0, 1)
            high_gu(0)
            high_x(3, 0, CT)
            exps(0, 1, 1)
            copy_qkv(1, 1)
            copy_probT(0, 1, 1)
            squares_1(1)
            high_gu(1)
            squares_2(0, 0, 1)
            copy_qkv(2, 0)
            squares_2(0, 1, 1)
            copy_qkv(2, 1)
            high_x2(0, 0, 1)
            copy_qkv(3, 0)
            high_x2(0, 1, 1)
            copy_qkv(3, 1)
            high_gu(2)
            high_gu(3)
            high_down(0)
            for g in range(GROUPS - 1):
                a, b = g + 1, g + 2
                tanh(g, 0)
                tanh(g, 1)
                if g == 0:
                    high_down(1)
                high_hidden(g, 0)
                high_hidden(g, 1)
                tanh(g, 2)
                exps(a, 0, CT)
                tanh(g, 3)
                high_hidden(g, 2)
                if b < GROUPS:
                    squares_1(b)
                tanh(g, 4)
                copy_probT(a, 0, CT)
                high_hidden(g, 3)
                tanh(g, 5)
                high_hidden(g, 4)
                tanh(g, 6)
                high_hidden(g, 5)
                high_hidden(g, 6)
                for c in range(CT):
                    squares_2(a, c, 1)
                tanh(g, 7)
                high_hidden(g, 7)
                for c in range(CT):
                    high_x2(a, c, 1)
            g = GROUPS - 1
            for m in range(CHUNKS):
                tanh(g, m)
                if m:
                    high_hidden(g, m - 1)
            high_hidden(g, CHUNKS - 1)

        @block.gpsimd
        def _(pool):
            def power_1(g):
                pool.wait_ge(ms1_ready, g + 1)
                if g:
                    pool.wait_ge(tab_ready, g)
                pool.tensor_tensor(rstd1[:, :], ms1[:, :], half_neg[:, :], ALU.pow).then_inc(rstd1_ready, 1)

            def power_2(g, c, n):
                pool.wait_ge(ms2_ready, done(g, c, n))
                if g:
                    pool.wait_ge(xn_ready, CT * g)
                pool.tensor_tensor(rstd2[:, c:c + n], ms2[:, c:c + n], half_neg[:, c:c + n],
                                   ALU.pow).then_inc(rstd2_ready, n)

            def low_hidden(g, m):
                n = g * CHUNKS + m
                pool.wait_ge(hf_hi, n + 1)
                pool.tensor_tensor(hf_l[:, m], hf[:, m], hf_h[:, m].bitcast(F32), ALU.subtract).then_inc(hf_lo, 1)

            def modulate_x(g):
                pool.wait_ge(in_xt[min(g, 2)], 16)
                modulate_tiles(pool, g, 0, CT).then_inc(hx_ready[1], CT)

            def low_x(g):
                pool.wait_ge(hx_hi, CT * (g + 1))
                low_tiles(pool, g, 0, CT).then_inc(hx_lo[1], CT)

            def low_gu(n):
                sl = slice(2 * n, 2 * n + 2)
                pool.wait_ge(wgu_hi, n + 1)
                pool.tensor_tensor(wgu_l[:, sl, :], wgu[:, sl, :], wgu_h[:, sl, :].bitcast(F32),
                                   ALU.subtract).then_inc(wgu_lo, 1)

            def low_down(n):
                sl = slice(4 * n, 4 * n + 4)
                pool.wait_ge(wd_hi, n + 1)
                pool.tensor_tensor(wd_l[:, sl, :], wd[:, sl, :], wd_h[:, sl, :].bitcast(F32),
                                   ALU.subtract).then_inc(wd_lo, 1)

            for k in range(KH):
                pool.wait_ge(wqkv_hi, k + 1)
                pool.tensor_tensor(wqkv_l[:, k, :], wqkv[:, k, :], wqkv_h[:, k, :].bitcast(F32),
                                   ALU.subtract).then_inc(wqkv_lo, 1)
            pool.wait_ge(half_ready, 1)
            power_1(0)
            pool.wait_ge(mod_ready[0], 1)
            modulate_x(1)
            modulate_x(2)
            low_x(1)
            low_x(2)
            modulate_x(3)
            low_gu(0)
            low_x(3)
            power_1(1)
            power_2(0, 0, 1)
            power_2(0, 1, 1)
            low_gu(1)
            low_gu(2)
            low_gu(3)
            low_down(0)
            for g in range(GROUPS - 1):
                a = g + 1
                for m in range(CHUNKS - 1):
                    low_hidden(g, m)
                    if g == 0 and m == 4:
                        low_down(1)
                    if m == 3 and a + 1 < GROUPS:
                        power_1(a + 1)
                power_2(a, 0, CT)
                low_hidden(g, CHUNKS - 1)
            for m in range(CHUNKS):
                low_hidden(GROUPS - 1, m)


def kernel(**inputs):
    import concourse.bacc as bacc
    from concourse.bass_utils import run_bass_kernel_spmd as run

    a = {n.replace("L0_cond_", ""): np.ascontiguousarray(v) for n, v in inputs.items()}

    def rows(w, parts):
        return w.reshape(parts, P, -1).transpose(1, 0, 2)

    x2d = a["x"].reshape(TOKENS, HIDDEN)
    xT = x2d.T.reshape(KH, P, GROUPS, GT).transpose(1, 2, 0, 3)
    x_tok = rows(x2d, TILES)
    pos = a["pos_BxS"].reshape(TILES, P).T
    batch_of = np.arange(P) // SEQ
    mask = (batch_of[:, None] == np.arange(BPT)[None, :]).astype(np.float32)
    exponent = np.arange(0, HD, 2, dtype=np.float32) / np.float32(HD)
    freq = np.broadcast_to(np.float32(1.0) / np.float32(ROPE_BASE) ** exponent, (P, HALF))
    pack_s = np.concatenate([a["ln1_w"].reshape(KH, P).T, a["ln2_w"].reshape(KH, P).T, mask, freq], axis=1)
    pack_a = np.concatenate([rows(a["cond_2048"].T, KH).reshape(P, -1), rows(a["ln1_tw"].T, KH).reshape(P, -1)], axis=1)
    w_qkv = rows(np.concatenate([a["Wq"], a["Wk"], a["Wv"]], axis=0).T, KH)
    pack_b = np.concatenate([np.eye(P, dtype=np.float32), rows(a["ln2_tw"].T, KH).reshape(P, -1),
                             rows(a["Wo"].T, HG).reshape(P, -1)], axis=1)
    w_gu = np.stack([a["Wg"], a["Wu"]]).reshape(2, CHUNKS, P, KH, P).transpose(4, 1, 0, 3, 2).reshape(P, CHUNKS, GU)
    w_d = rows(a["Wd"].T, CHUNKS)

    nc = bacc.Bacc("TRN2", target_bir_lowering=False, num_devices=1)
    arrays, args = {}, []
    for name, v in (("xT", xT), ("x_tok", x_tok), ("pos", pos), ("pack_s", pack_s), ("pack_a", pack_a), ("w_qkv", w_qkv),
                    ("pack_b", pack_b), ("w_gu", w_gu), ("w_d", w_d)):
        v = np.ascontiguousarray(v)
        arrays["in_" + name] = v
        args.append(nc.dram_tensor("in_" + name, v.shape, mybir.dt.from_np(v.dtype), kind="ExternalInput").ap())
    args.append(nc.dram_tensor("out_x", (TOKENS, HIDDEN), F32, kind="ExternalOutput").ap())
    block_program(nc, *args)
    r = run(nc, [arrays], core_ids=[0])
    return r.results[0]["out_x"].reshape(BATCH, SEQ, HIDDEN)
```
